# Optimizing a Trainium2 kernel written in Bass

```python
import numpy as np
import jax
import jax.numpy as jnp

def _softmax(x, axis=-1):
    return jax.nn.softmax(x, axis=axis)

def _gelu(x):
    return jax.nn.gelu(x, approximate=True)

def _silu(x):
    return jax.nn.silu(x)

def _sigmoid(x):
    return jax.nn.sigmoid(x)

def _layernorm(x, axis=-1, eps=1e-05):
    m = jnp.mean(x, axis=axis, keepdims=True)
    v = jnp.var(x, axis=axis, keepdims=True)
    return (x - m) / jnp.sqrt(v + eps)

def _scatter_add(tgt, idx, src, axis=0):
    return tgt.at[idx].add(src)

def _segment_sum(src, seg, n):
    return jax.ops.segment_sum(src, seg, n)
kernel_name = 'mk_flamingo_gated_d2_seqx_r4_8155ad'

def setup_inputs(seed: int=0):
    np.random.seed(seed)
    _w = jnp.asarray

    def _rec_inputs():
        import jax
        import jax.numpy as jnp
        _rk = jax.random.key(seed)
        x = -0.0002928 + 1 * jax.random.normal(jax.random.fold_in(_rk, 1), (8, 256, 256), jnp.float32)
        _lenS = 256 - jax.random.randint(jax.random.fold_in(_rk, 7), (8,), 0, max(1, 256 // 4) + 1, jnp.int32)
        _lenS2 = 256 - jax.random.randint(jax.random.fold_in(_rk, 8), (8,), 0, max(1, 256 // 4) + 1, jnp.int32)
        _ctx_1024P = jax.random.normal(jax.random.fold_in(_rk, 11), (8, 16, 256), jnp.float32)
        _ctx_1024c = jax.random.dirichlet(jax.random.fold_in(_rk, 511), 0.3 * jnp.ones((16,), jnp.float32), (8, 256))
        _ctx_1024t = jnp.einsum('bsk,bkd->bsd', _ctx_1024c, _ctx_1024P)
        _ctx_1024t = _ctx_1024t * jax.lax.rsqrt(jnp.mean(jnp.square(_ctx_1024t)) + 1e-12) * 0.953939
        ctx_1024 = -1.39393e-06 + 0.999914 * (_ctx_1024t + 0.3 * jax.random.normal(jax.random.fold_in(_rk, 611), (8, 256, 256), jnp.float32))
        _g = jax.random.normal(jax.random.fold_in(_rk, 9001), (2, 2), jnp.float32)
        _g = jnp.sign(_g) * jnp.maximum(jnp.abs(_g), 1.0) + (_g == 0) * 1.0
        g_xattn = _g[0]
        g_ffn = _g[1]
        return (x, ctx_1024, g_xattn, g_ffn)
    x, ctx_1024, g_xattn, g_ffn = _rec_inputs()

    def _L0_xattn_setup():
        import jax, jax.numpy as jnp
        import numpy as np
        B, S, D = (2, 512, 256)
        H = 16
        CHUNK = 64
        NEG_INF = -1000000000.0
        key = jax.random.key(seed)
        ks = jax.random.split(key, 11)
        std = 1.0 / np.sqrt(D)
        return {'query': jax.random.normal(ks[0], (B, S, D), jnp.float32), 'key': jax.random.normal(ks[1], (B, S, D), jnp.float32), 'value': jax.random.normal(ks[2], (B, S, D), jnp.float32), 'Wq': jax.random.normal(ks[3], (D, D), jnp.float32) * std, 'bq': jax.random.normal(ks[4], (D,), jnp.float32) * 0.01, 'Wk': jax.random.normal(ks[5], (D, D), jnp.float32) * std, 'bk': jax.random.normal(ks[6], (D,), jnp.float32) * 0.01, 'Wv': jax.random.normal(ks[7], (D, D), jnp.float32) * std, 'bv': jax.random.normal(ks[8], (D,), jnp.float32) * 0.01, 'Wo': jax.random.normal(ks[9], (D, D), jnp.float32) * std, 'bo': jax.random.normal(ks[10], (D,), jnp.float32) * 0.01}
    _L0_xattn_all = _L0_xattn_setup()
    _L0_xattn_in = {k: v for k, v in _L0_xattn_all.items() if k in ('Wq', 'bq', 'Wk', 'bk', 'Wv', 'bv', 'Wo', 'bo')}
    del _L0_xattn_all

    def _L0_ffn_setup():
        import jax, jax.numpy as jnp
        import numpy as np
        DIM = 256
        HIDDEN = 512
        N_EXPERTS = 8
        TOP_K = 2
        EPS = 1e-06

        def rms_norm(x, scale, eps=EPS):
            ms = jnp.mean(jnp.square(x.astype(jnp.float32)), axis=-1, keepdims=True)
            s = scale.astype(jnp.float32) * jax.lax.rsqrt(ms + eps)
            return x * s.astype(x.dtype)

        def moe_linear(xf, ids, W):
            E = W.shape[0]
            out = jnp.zeros((xf.shape[0], W.shape[1]), dtype=xf.dtype)
            for e in range(E):
                out = out + jnp.where((ids == e)[:, None], xf @ W[e].T, 0.0)
            return out
        key = jax.random.key(seed)
        k1, k2, k3, k4 = jax.random.split(key, 4)
        x = jax.random.normal(k1, (4, 1024, DIM), dtype=jnp.float32)
        norm_scale = jnp.ones((DIM,), dtype=jnp.float32)
        w_router = jax.random.normal(k2, (N_EXPERTS, DIM), dtype=jnp.float32) / np.sqrt(DIM)
        lim_up = np.sqrt(6.0 / (DIM + 2 * HIDDEN))
        w_up = jax.random.uniform(k3, (N_EXPERTS, 2 * HIDDEN, DIM), dtype=jnp.float32, minval=-lim_up, maxval=lim_up)
        lim_dn = np.sqrt(6.0 / (HIDDEN + DIM))
        w_down = jax.random.uniform(k4, (N_EXPERTS, DIM, HIDDEN), dtype=jnp.float32, minval=-lim_dn, maxval=lim_dn)
        return {'x': x, 'norm_scale': norm_scale, 'w_router': w_router, 'w_up': w_up, 'w_down': w_down}
    _L0_ffn_all = _L0_ffn_setup()
    _L0_ffn_in = {k: v for k, v in _L0_ffn_all.items() if k in ('norm_scale', 'w_router', 'w_up', 'w_down')}
    del _L0_ffn_all

    def _L1_xattn_setup():
        import jax, jax.numpy as jnp
        import numpy as np
        HEADS = 16
        DIM_HEAD = 64
        SCALE = DIM_HEAD ** (-0.5)

        def _split_heads(x):
            b, l, n = x.shape
            return x.reshape(b, l, HEADS, DIM_HEAD).transpose(0, 2, 1, 3)
        key = jax.random.key(seed)
        ks = jax.random.split(key, 6)
        B, L, D = (4, 512, 256)
        inner = HEADS * DIM_HEAD
        s = lambda fan_in: 1.0 / np.sqrt(fan_in)
        return {'x1': jax.random.normal(ks[0], (B, L, D), jnp.float32), 'x2': jax.random.normal(ks[1], (B, L, D), jnp.float32), 'Wq': jax.random.normal(ks[2], (D, inner), jnp.float32) * s(D), 'Wkv': jax.random.normal(ks[3], (D, 2 * inner), jnp.float32) * s(D), 'Wo': jax.random.normal(ks[4], (inner, D), jnp.float32) * s(inner), 'bo': jax.random.normal(ks[5], (D,), jnp.float32) * 0.02}
    _L1_xattn_all = _L1_xattn_setup()
    _L1_xattn_in = {k: v for k, v in _L1_xattn_all.items() if k in ('Wq', 'Wkv', 'Wo', 'bo')}
    del _L1_xattn_all

    def _L1_ffn_setup():
        import jax, jax.numpy as jnp
        import numpy as np
        B, S, D_MODEL, D_FF, E, R, TOP_K = (4, 512, 256, 1024, 8, 16, 2)
        key = jax.random.key(seed)
        ks = jax.random.split(key, 9)
        sd = 1.0 / np.sqrt(D_MODEL)
        return {'hidden_states': jax.random.normal(ks[0], (B, S, D_MODEL), jnp.float32), 'wi': jax.random.normal(ks[1], (D_FF, D_MODEL), jnp.float32) * sd, 'bi': jax.random.normal(ks[2], (D_FF,), jnp.float32) * 0.01, 'wo': jax.random.normal(ks[3], (D_MODEL, D_FF), jnp.float32) * (1.0 / np.sqrt(D_FF)), 'bo': jax.random.normal(ks[4], (D_MODEL,), jnp.float32) * 0.01, 'lora_A': jax.random.normal(ks[5], (E, R, D_MODEL), jnp.float32) * sd, 'lora_B': jax.random.normal(ks[6], (E, D_FF, R), jnp.float32) * 0.02, 'gate_w': jax.random.normal(ks[7], (E, D_MODEL), jnp.float32) * sd, 'gate_b': jax.random.normal(ks[8], (E,), jnp.float32) * 0.01}
    _L1_ffn_all = _L1_ffn_setup()
    _L1_ffn_in = {k: v for k, v in _L1_ffn_all.items() if k in ('wi', 'bi', 'wo', 'bo', 'lora_A', 'lora_B', 'gate_w', 'gate_b')}
    del _L1_ffn_all
    return {'x': x, 'ctx_1024': ctx_1024, 'g_xattn': g_xattn, 'g_ffn': g_ffn, 'L0_xattn_Wq': _L0_xattn_in['Wq'], 'L0_xattn_bq': _L0_xattn_in['bq'], 'L0_xattn_Wk': _L0_xattn_in['Wk'], 'L0_xattn_bk': _L0_xattn_in['bk'], 'L0_xattn_Wv': _L0_xattn_in['Wv'], 'L0_xattn_bv': _L0_xattn_in['bv'], 'L0_xattn_Wo': _L0_xattn_in['Wo'], 'L0_xattn_bo': _L0_xattn_in['bo'], 'L0_ffn_norm_scale': _L0_ffn_in['norm_scale'], 'L0_ffn_w_router': _L0_ffn_in['w_router'], 'L0_ffn_w_up': _L0_ffn_in['w_up'], 'L0_ffn_w_down': _L0_ffn_in['w_down'], 'L1_xattn_Wq': _L1_xattn_in['Wq'], 'L1_xattn_Wkv': _L1_xattn_in['Wkv'], 'L1_xattn_Wo': _L1_xattn_in['Wo'], 'L1_xattn_bo': _L1_xattn_in['bo'], 'L1_ffn_wi': _L1_ffn_in['wi'], 'L1_ffn_bi': _L1_ffn_in['bi'], 'L1_ffn_wo': _L1_ffn_in['wo'], 'L1_ffn_bo': _L1_ffn_in['bo'], 'L1_ffn_lora_A': _L1_ffn_in['lora_A'], 'L1_ffn_lora_B': _L1_ffn_in['lora_B'], 'L1_ffn_gate_w': _L1_ffn_in['gate_w'], 'L1_ffn_gate_b': _L1_ffn_in['gate_b']}

def reference(x, ctx_1024, g_xattn, g_ffn, L0_xattn_Wq, L0_xattn_bq, L0_xattn_Wk, L0_xattn_bk, L0_xattn_Wv, L0_xattn_bv, L0_xattn_Wo, L0_xattn_bo, L0_ffn_norm_scale, L0_ffn_w_router, L0_ffn_w_up, L0_ffn_w_down, L1_xattn_Wq, L1_xattn_Wkv, L1_xattn_Wo, L1_xattn_bo, L1_ffn_wi, L1_ffn_bi, L1_ffn_wo, L1_ffn_bo, L1_ffn_lora_A, L1_ffn_lora_B, L1_ffn_gate_w, L1_ffn_gate_b):
    import jax
    import jax.numpy as jnp

    def _L0_xattn_ref(query, key, value, Wq, bq, Wk, bk, Wv, bv, Wo, bo):
        import jax, jax.numpy as jnp
        import numpy as np
        B, S, D = (2, 512, 256)
        H = 16
        CHUNK = 64
        NEG_INF = -1000000000.0
        b, s, d = query.shape
        hd = d // H
        scale = 1.0 / jnp.sqrt(jnp.asarray(hd, query.dtype))
        q = (query @ Wq + bq).reshape(b, s, H, hd)
        k = (key @ Wk + bk).reshape(b, s, H, hd)
        v = (value @ Wv + bv).reshape(b, s, H, hd)
        scores = jnp.einsum('bqhd,bkhd->bhqk', q, k) * scale
        pos = jnp.arange(s)
        block_end = (pos // CHUNK + 1) * CHUNK
        mask = pos[None, :] < block_end[:, None]
        scores = jnp.where(mask[None, None], scores, NEG_INF)
        attn = jax.nn.softmax(scores, axis=-1)
        out = jnp.einsum('bhqk,bkhd->bqhd', attn, v).reshape(b, s, d)
        return out @ Wo + bo

    def _L0_ffn_ref(x, norm_scale, w_router, w_up, w_down):
        import jax, jax.numpy as jnp
        import numpy as np
        DIM = 256
        HIDDEN = 512
        N_EXPERTS = 8
        TOP_K = 2
        EPS = 1e-06

        def rms_norm(x, scale, eps=EPS):
            ms = jnp.mean(jnp.square(x.astype(jnp.float32)), axis=-1, keepdims=True)
            s = scale.astype(jnp.float32) * jax.lax.rsqrt(ms + eps)
            return x * s.astype(x.dtype)

        def moe_linear(xf, ids, W):
            E = W.shape[0]
            out = jnp.zeros((xf.shape[0], W.shape[1]), dtype=xf.dtype)
            for e in range(E):
                out = out + jnp.where((ids == e)[:, None], xf @ W[e].T, 0.0)
            return out
        B, S, D = x.shape
        skip = x
        xn = rms_norm(x, norm_scale)
        scores = (xn @ w_router.T).astype(jnp.float32)
        scores_topk, idx = jax.lax.top_k(scores, TOP_K)
        weights = jax.nn.softmax(scores_topk, axis=-1)
        xf = jnp.broadcast_to(xn[..., None, :], (B, S, TOP_K, D)).reshape(-1, D)
        ids = idx.reshape(-1)
        up = moe_linear(xf, ids, w_up)
        u, gate = jnp.split(up, 2, axis=-1)
        h = u * jax.nn.silu(gate)
        down = moe_linear(h, ids, w_down)
        down = down.reshape(B, S, TOP_K, D)
        out = jnp.sum(down * weights[..., None].astype(down.dtype), axis=-2)
        return out + skip

    def _L1_xattn_ref(x1, x2, Wq, Wkv, Wo, bo):
        import jax, jax.numpy as jnp
        import numpy as np
        HEADS = 16
        DIM_HEAD = 64
        SCALE = DIM_HEAD ** (-0.5)

        def _split_heads(x):
            b, l, n = x.shape
            return x.reshape(b, l, HEADS, DIM_HEAD).transpose(0, 2, 1, 3)
        q = x1 @ Wq
        kv = x2 @ Wkv
        k, v = jnp.split(kv, 2, axis=-1)
        q, k, v = map(_split_heads, (q, k, v))
        attn = jnp.einsum('bhid,bhjd->bhij', q, k) * SCALE
        attn = jax.nn.softmax(attn, axis=-1)
        out = jnp.einsum('bhij,bhjd->bhid', attn, v)
        b, h, l, d = out.shape
        out = out.transpose(0, 2, 1, 3).reshape(b, l, h * d)
        return out @ Wo + bo

    def _L1_ffn_ref(hidden_states, wi, bi, wo, bo, lora_A, lora_B, gate_w, gate_b):
        import jax, jax.numpy as jnp
        import numpy as np
        B, S, D_MODEL, D_FF, E, R, TOP_K = (4, 512, 256, 1024, 8, 16, 2)
        logits = jnp.einsum('bsd,ed->bse', hidden_states, gate_w) + gate_b
        scores = jax.nn.softmax(logits, axis=-1)
        top_v, top_i = jax.lax.top_k(scores, TOP_K)
        val_sum = top_v.sum(axis=-1)
        out = jnp.zeros_like(hidden_states)
        for e in range(E):
            count = (top_i == e).sum(axis=-1).astype(hidden_states.dtype)
            gate = count * val_sum
            inter = jnp.einsum('bsd,fd->bsf', hidden_states, wi) + bi + jnp.einsum('bsr,fr->bsf', jnp.einsum('bsd,rd->bsr', hidden_states, lora_A[e]), lora_B[e])
            h = jax.nn.relu(inter)
            expert_out = jnp.einsum('bsf,df->bsd', h, wo) + bo
            out = out + gate[..., None] * expert_out
        return out
    x = x + jnp.tanh(g_xattn[0]) * _L0_xattn_ref(_layernorm(x, axis=-1), ctx_1024, ctx_1024, L0_xattn_Wq, L0_xattn_bq, L0_xattn_Wk, L0_xattn_bk, L0_xattn_Wv, L0_xattn_bv, L0_xattn_Wo, L0_xattn_bo)
    x = x + jnp.tanh(g_ffn[0]) * _L0_ffn_ref(_layernorm(x, axis=-1), L0_ffn_norm_scale, L0_ffn_w_router, L0_ffn_w_up, L0_ffn_w_down)
    x = x + jnp.tanh(g_xattn[1]) * _L1_xattn_ref(_layernorm(x, axis=-1), ctx_1024, L1_xattn_Wq, L1_xattn_Wkv, L1_xattn_Wo, L1_xattn_bo)
    x = x + jnp.tanh(g_ffn[1]) * _L1_ffn_ref(_layernorm(x, axis=-1), L1_ffn_wi, L1_ffn_bi, L1_ffn_wo, L1_ffn_bo, L1_ffn_lora_A, L1_ffn_lora_B, L1_ffn_gate_w, L1_ffn_gate_b)
    return x

_drawn_inputs = setup_inputs


def setup_inputs(seed=0):
    import zlib

    import numpy as np

    out = dict(_drawn_inputs(seed))
    spreads = {'g_ffn': (-1.0, 0.2), 'L0_ffn_norm_scale': (1.0, 0.2)}
    factors = {'L0_xattn_bq': 8.0,
     'L0_xattn_bk': 8.0,
     'L0_xattn_bv': 3.514,
     'L0_xattn_bo': 3.984,
     'L1_ffn_bi': 7.74,
     'L1_ffn_bo': 5.535,
     'L1_ffn_gate_b': 8.0}
    for name, (base, spread) in spreads.items():
        noise = np.random.default_rng([zlib.crc32(name.encode()), seed]).standard_normal(out[name].shape)
        drawn = base * np.exp(spread * noise) if base else spread * noise
        out[name] = jnp.asarray(drawn.astype(out[name].dtype))
    for name, factor in factors.items():
        out[name] = (out[name] * factor).astype(out[name].dtype)
    return out
```

```python
from contextlib import ExitStack

import numpy as np

import concourse.bass as bass
from concourse import mybir
from concourse.alu_op_type import AluOpType as ALU

ACT = mybir.ActivationFunctionType
F32 = mybir.dt.float32
BF16 = mybir.dt.bfloat16
I32 = mybir.dt.int32
U32 = mybir.dt.uint32
AX = mybir.AxisListType

P = 128
B, S, D = 8, 256, 256
TT = S // P
DC = D // P
NT = B * TT
NH = 16
HD0, HD1 = 16, 64
SLOT0 = 32
G0, G1 = 4, 2
CHUNK = 64
E = 8
HID = 512
FF = 1024
FC = FF // P
HC = HID // P
R = 16
CAP = S * B + P
PAD_ROW = E * CAP
TILES = (2 * S * B + E * (P - 1)) // P
ROWS_IN, ROWS_OUT = PAD_ROW + P, TILES * P
NPT = 8
LN_EPS, RMS_EPS = 1e-5, 1e-6
NEG = -1e9
LOWER = -1e30

PROJ_A = ["xT", "qk0", "v0", "qk1", "v1"]
POST_A = ["rT", "bc0", "bc1", "wo", "x2T", "rt", "rank"]
SCHED_A = [(1, "proj", "qk1", 0), (5, "proj", "v1", 0), (7, "proj", "xT", 1), (10, "proj", "qk0", 1),
           (11, "proj", "v0", 1), (3, "post", "rT", -1), (4, "post", "bc0", -1), (4, "post", "bc1", -1),
           (6, "post", "wo", -1), (9, "post", "x2T", -1), (10, "post", "rt", -1), (12, "post", "rank", -1)]
PROJ_C = ["xT"] + [f"{w}{p}" for p in range(8) for w in ("qk", "v")]
POST_C = (["rT"] + [f"bc{j}" for j in range(4)] + ["wo", "x3T", "rt", "la", "laT"] + [f"up{c}" for c in range(FC)]
          + ["down"])
SCHED_C = ([(2 * j, "proj", f"qk{j + 1}", 0) for j in range(7)] + [(2 * j + 1, "proj", f"v{j + 1}", 0) for j in range(7)]
           + [(13, "proj", "xT", 1)]
           + [(s, "post", j, -1) for s, j in zip([3, 4, 4, 5, 5, 6, 8, 9, 9, 12, 13, 13, 13, 14, 14, 14, 15, 15, 15], POST_C)]
           + [(14, "proj", "qk0", 1), (15, "proj", "v0", 1)])
SCATTER_SLOTS = {13: (0,), 14: (1,), 15: (2, 3)}


class Family:

    def __init__(self, names, banks, ready, taken):
        self.names, self.banks, self.ready, self.taken = names, banks, ready, taken

    def place(self, job, batch):
        j, n = self.names.index(job), len(self.banks)
        k = j % n
        return k, batch * ((len(self.names) - k + n - 1) // n) + j // n

    def bank(self, job):
        return self.banks[self.names.index(job) % len(self.banks)]

    def wait_free(self, eng, job, batch):
        k, n = self.place(job, batch)
        eng.wait_ge(self.taken[k], n + 1)

    def wait_ready(self, eng, job, batch):
        k, n = self.place(job, batch)
        eng.wait_ge(self.ready[k], n + 1)

    def wait_taken(self, eng, job, batch):
        k, n = self.place(job, batch)
        eng.wait_ge(self.taken[k], n + 2)

    def wait_other(self, eng, job, other, batch):
        if self.bank(job) is not self.bank(other):
            self.wait_taken(eng, other, batch)

    def ready_of(self, job):
        return self.ready[self.names.index(job) % len(self.banks)]

    def taken_of(self, job):
        return self.taken[self.names.index(job) % len(self.banks)]


def due(sched, slot, b, post, own, front):
    return [(f, j, b + d) for s, f, j, d in sched if s == slot and (post, own, front)[d + 1]]


class Steps:

    def __init__(self, eng, sem):
        self.eng, self.sem, self.n, self.turn = eng, sem, 0, 0

    def loop(self, i, per):
        self.turn, self.per, self.n0 = i * per, per, self.n

    def end(self, times):
        assert self.n - self.n0 == self.per, (self.n - self.n0, self.per)
        self.n, self.turn = self.n0 + times * self.per, 0

    def done(self, ins):
        ins.then_inc(self.sem, 1)
        self.n += 1
        self.eng.wait_ge(self.sem, self.n + self.turn)

    def hold(self):
        self.eng.sem_inc(self.sem, 1)
        self.n += 1


def columns(x, n):
    return x.broadcast_to([x.shape[0], n])


def build(nc, x, ctxT, g_x, g_f, Wq0, bq0, Wk0, bk0, Wv0, bv0, Wo0, bo0, nscale, w_routerT, w_upT, w_downT,
          Wq1, Wkv1, Wo1, bo1, wiT, bi, woT, bo3, loraAT, loraB, gate_wT, gate_b, out):
    with ExitStack() as whole:
        whole.enter_context(nc.allow_non_contiguous_dma(reason="small vectors onto partitions"))
        sem = lambda name: whole.enter_context(nc.semaphore(name))
        keep = lambda name, shape, dt=F32: whole.enter_context(nc.sbuf_tensor(name, shape, dt))
        bank = [whole.enter_context(nc.psum_tensor(f"bank{i}", [P, 512], F32)) for i in range(8)]
        rows_in = nc.dram_tensor("rows_in", [ROWS_IN, D], F32, kind="Internal").ap()
        rows_out = nc.dram_tensor("rows_out", [ROWS_OUT, D], F32, kind="Internal").ap()

        x_all = keep("x_all", [P, NT, D])
        w_up = keep("w_up", [P, E * DC * 2 * HID])
        w_dn = keep("w_dn", [P, E * HC * D])
        ident = keep("ident", [P, P])
        gates = keep("gates", [P, 4])
        ns = keep("ns", [P, DC])
        gap = keep("gap", [P, NT])
        mix = keep("mix", [P, 2, NT])
        pos_all = keep("pos_all", [P, 2, NT], U32)
        base = keep("base", [P, E])
        row_tab = keep("row_tab", [1, 40], I32)
        exp_tab = keep("exp_tab", [1, 40], I32)
        nhalf = keep("nhalf", [P, TT])
        tab = keep("tab", [P, 40 * E])
        tab2 = keep("tab2", [P, 40 * E])
        small = keep("small", [P, 160])

        w_up_v = w_up[:].rearrange("p (e c h) -> p e c h", e=E, c=DC)
        w_dn_v = w_dn[:].rearrange("p (e c h) -> p e c h", e=E, c=HC)

        moe_loaded = sem("moe_loaded")
        pads_done = sem("pads_done")
        scattered = sem("scattered")
        tables_done = sem("tables_done")
        mixes_done = sem("mixes_done")

        phase_a(nc, locals())
        phase_bc(nc, locals())


def phase_a(nc, v):
    x, ctxT, x_all, bank, ident, gates, ns = (v[k] for k in ("x", "ctxT", "x_all", "bank", "ident", "gates", "ns"))
    gap, mix, pos_all, base, row_tab, exp_tab, nhalf, tab, tab2, small = (v[k] for k in (
        "gap", "mix", "pos_all", "base", "row_tab", "exp_tab", "nhalf", "tab", "tab2", "small"))
    rows_in = v["rows_in"]
    moe_loaded, pads_done, scattered, tables_done, mixes_done = (v[k] for k in (
        "moe_loaded", "pads_done", "scattered", "tables_done", "mixes_done"))
    with ExitStack() as ctx:
        sb = lambda name, shape, dt=F32: ctx.enter_context(nc.sbuf_tensor(name, shape, dt))
        sem = lambda name: ctx.enter_context(nc.semaphore(name))

        wq, wk, wv = (sb(n, [P, DC, D]) for n in ("wq0", "wk0", "wv0"))
        wo = sb("wo0", [P, G0, D])
        bvs = sb("bvs", [P, G0])
        bvb = sb("bvb", [P, G0, P])
        bqk = sb("bqk0", [P, 2, DC])
        wr = sb("wr", [P, DC, E])
        crow = sb("crow0", [P, D])
        head_mask = sb("head_mask", [P, E])
        sel = sb("sel0", [NH, G0, P])
        tri = sb("tri", [P, P], BF16)
        ones = sb("ones", [P, P], BF16)
        mrow = sb("mrow", [1, P], BF16)
        mneg = sb("mneg", [1, CHUNK], BF16)
        rev = sb("rev", [P, TT, E])
        xn = sb("xn0", [P, TT, D])
        xnT = sb("xnT0", [P, DC, S])
        cT = sb("cT0", [P, DC, S])
        qT = sb("qT0", [P, DC, S])
        kT = sb("kT0", [P, DC, S])
        qz = sb("qz", [P, 4, S])
        V = sb("V0", [P, TT, NH, SLOT0])
        prob = sb("prob0", [P, 2, 384])
        pT = sb("pT0", [P, NPT, 384])
        nmax = sb("nmax0", [P, 4, TT])
        den = sb("den0", [P, TT, NH])
        rinv = sb("rinv0", [P, TT, NH])
        rT = sb("rT0", [NH, S])
        oT = sb("oT0", [P, G0, S])
        oTn = sb("oTn0", [P, G0, S])
        st = sb("st0", [P, TT, 6])
        mv = sb("mv0", [P, TT, 2])
        st2 = sb("st02", [P, TT, 6])
        mv2 = sb("mv02", [P, TT, 2])
        lnw = sb("lnw0", [P, 2, TT])
        lnw2 = sb("lnw02", [P, 6, TT])
        xp = sb("xp", [P, TT, D])
        xs = sb("xs", [P, TT, D])
        xt = sb("xt0", [P, TT, D])
        x2T = sb("x2T", [P, DC, S])
        lg = sb("lg0", [P, TT, E])
        rw = sb("rw0", [P, 8, TT * E])
        r1 = sb("r10", [P, 4, TT])
        oh = sb("oh0", [P, 2, TT * E])
        hot = sb("hot", [P, TT * E], BF16)
        pos4 = sb("pos4", [P, 2 * TT], U32)
        posf = sb("posf", [P, 2, TT])
        credit = sb("credit", [P, 4])
        zrow = sb("zrow", [P, D])
        padf = sb("padf", [P, E])
        padi = sb("padi", [P, E], U32)

        w_loaded = sem("w_loaded")
        wo_loaded = sem("wo_loaded")
        x0_loaded, x_loaded, ctx_loaded = sem("x0_loaded"), sem("x_loaded"), sem("ctx_loaded")
        small_loaded = sem("small_loaded")
        consts_done = sem("consts_done")
        zeroed = sem("zeroed")
        gates_done = sem("gates_done")
        crow_done = sem("crow_done")
        bvb_done = sem("bvb_done")
        scores_ready, nmax_ready, probs_ready = sem("scores_ready"), sem("nmax_ready"), sem("probs_ready")
        pT_ready, pT_taken = sem("pT_ready"), sem("pT_taken")
        out_ready, out_taken = sem("out_ready"), sem("out_taken")
        qz_ready, rinv_ready = sem("qz_ready"), sem("rinv_ready")
        stats_ready, xn_ready, x_shifted = sem("stats_ready"), sem("xn_ready"), sem("x_shifted")
        root_ready, root2_ready = sem("root_ready"), sem("root2_ready")
        xt_ready, xp_used = sem("xt_ready"), sem("xp_used")
        stats2_ready, xs_ready = sem("stats2_ready"), sem("xs_ready")
        hot_ready, pos_ready = sem("hot_ready"), sem("pos_ready")
        vec_step, pool_step, act_step = sem("vec_step_a"), sem("pool_step_a"), sem("act_step_a")

        S_BANK, T_BANK, O_BANK = bank[0:2], bank[2:4], bank[4:6]
        fam = {"proj": Family(PROJ_A, [bank[6]], [sem("proj_ready")], [sem("proj_taken")]),
               "post": Family(POST_A, [bank[7]], [sem("post_ready")], [sem("post_taken")])}
        crow_ready = sem("crow_ready")
        CONSTS = 9
        block = ctx.enter_context(nc.Block())

        @block.sync
        def _(sp):
            xv = x.rearrange("b (t p) d -> p (b t) d", p=P)
            cv = ctxT.rearrange("b (c p) s -> b p c s", p=P)
            sp.dma_start(x_all[:, 0:TT, :], xv[:, 0:TT, :]).then_inc(x0_loaded, 16)
            sp.dma_start(cT[:], cv[0]).then_inc(ctx_loaded, 16)
            for t, w in ((wq, v["Wq0"]), (wk, v["Wk0"]), (wv, v["Wv0"])):
                sp.dma_start(t[:], w.rearrange("(c p) n -> p c n", p=P)).then_inc(w_loaded, 16)
            for j, w in enumerate((v["bq0"], v["bk0"])):
                sp.dma_start(bqk[:, j, :], w.rearrange("(c p) -> p c", p=P)).then_inc(w_loaded, 16)
            sp.dma_start(x_all[:, TT:NT, :], xv[:, TT:NT, :]).then_inc(x_loaded, 16)
            sp.dma_start(wr[:], v["w_routerT"].rearrange("(c p) n -> p c n", p=P)).then_inc(w_loaded, 16)
            for e in range(E):
                sp.dma_start(v["w_up_v"][:, e], v["w_upT"][e].rearrange("(c p) h -> p c h", p=P)).then_inc(moe_loaded, 16)
                sp.dma_start(v["w_dn_v"][:, e], v["w_downT"][e].rearrange("(c p) d -> p c d", p=P)).then_inc(moe_loaded, 16)

            def next_context(b):
                fam["proj"].wait_ready(sp, "v1", b)
                sp.dma_start(cT[:], cv[bass.ds(b + 1, 1)].rearrange("o p c s -> (o p) c s")).then_inc(ctx_loaded, 16)

            next_context(0)
            with sp.Fori(1, B - 1) as b:
                next_context(b)

        @block.gpsimd
        def _(pool):
            step = Steps(pool, pool_step)
            pool.dma_start(gates[:, 0:2], v["g_x"].partition_broadcast(P)).then_inc(small_loaded, 16)
            pool.dma_start(gates[:, 2:4], v["g_f"].partition_broadcast(P)).then_inc(small_loaded, 16)
            pool.dma_start(ns[:], v["nscale"].rearrange("(c p) -> p c", p=P)).then_inc(small_loaded, 16)
            pool.dma_start(crow[:], v["bo0"].partition_broadcast(P)).then_inc(small_loaded, 16)
            pool.wait_ge(zeroed, 2)
            bvv = v["bv0"].rearrange("(h d) -> d h", d=HD0)
            for j in range(G0):
                pool.dma_start(wo[SLOT0 * j:SLOT0 * j + HD0, :, :],
                               v["Wo0"].rearrange("(g j d) n -> j d g n", j=G0, d=HD0)[j]).then_inc(wo_loaded, 16)
                pool.dma_start(bvs[SLOT0 * j:SLOT0 * j + HD0, :], bvv[:, j:NH:G0]).then_inc(wo_loaded, 16)

            pool.memset(nhalf[:], -0.5).then_inc(consts_done, 1)
            step.done(pool.memset(ident[:], 1.0))
            pool.affine_select(out=ident[:], in_=ident[:], compare_op=ALU.is_equal, fill=0.0, base=0,
                               pattern=[[-1, P]], channel_multiplier=1).then_inc(consts_done, 1)
            step.done(pool.memset(head_mask[:], HD0 ** -0.5))
            step.done(pool.affine_select(out=head_mask[:], in_=head_mask[:], compare_op=ALU.is_ge, fill=0.0, base=0,
                                         pattern=[[-HD0, E]], channel_multiplier=1))
            pool.affine_select(out=head_mask[:], in_=head_mask[:], compare_op=ALU.is_ge, fill=0.0, base=HD0 - 1,
                               pattern=[[HD0, E]], channel_multiplier=-1).then_inc(consts_done, 1)
            step.done(pool.memset(sel[:], 1.0))
            pool.affine_select(out=sel[:].rearrange("h g (j d) -> h g j d", j=G0), in_=sel[:].rearrange(
                "h g (j d) -> h g j d", j=G0), compare_op=ALU.is_equal, fill=0.0, base=0,
                pattern=[[-G0, G0], [-1, G0], [0, SLOT0]], channel_multiplier=1).then_inc(consts_done, 1)
            pool.memset(ones[:], 1.0).then_inc(consts_done, 1)
            step.done(pool.memset(tri[:], 1.0))
            pool.affine_select(out=tri[:], in_=tri[:], compare_op=ALU.is_gt, fill=0.0, base=0,
                               pattern=[[1, P]], channel_multiplier=-1).then_inc(consts_done, 1)
            step.done(pool.memset(mrow[:], 0.0))
            pool.memset(mrow[:, 0:CHUNK], 1.0).then_inc(consts_done, 1)
            pool.memset(mneg[:], NEG).then_inc(consts_done, 1)
            pool.iota(rev[:], pattern=[[0, TT], [-1, E]], base=E, channel_multiplier=0,
                      allow_small_or_imprecise_dtypes=True).then_inc(consts_done, 1)
            pool.iota(base[:], pattern=[[CAP, E]], base=0, channel_multiplier=0,
                      allow_small_or_imprecise_dtypes=True)
            pool.iota(tab[:, 0:E * 16].rearrange("p (e j) -> p e j", j=16), pattern=[[0, E], [P, 16]], base=0,
                      channel_multiplier=0, allow_small_or_imprecise_dtypes=True)
            pool.iota(tab2[:].rearrange("p (i e) -> p i e", e=E), pattern=[[1, 40], [0, E]], base=0,
                      channel_multiplier=0, allow_small_or_imprecise_dtypes=True)
            pool.iota(small[:, 0:40], pattern=[[P, 40]], base=0, channel_multiplier=0,
                      allow_small_or_imprecise_dtypes=True)
            pool.iota(padf[:], pattern=[[0, E]], base=0, channel_multiplier=1,
                      allow_small_or_imprecise_dtypes=True).then_inc(tables_done, 1)

            def root(w, m, eps):
                step.hold()
                step.done(pool.tensor_scalar(w[:, 0, :], m[:, :, 1], eps, None, ALU.add))
                return pool.tensor_tensor(w[:, 1, :], w[:, 0, :], nhalf[:], ALU.pow)

            def front_root(b1):
                pool.wait_ge(stats_ready, b1 + 1)
                root(lnw, mv, LN_EPS).then_inc(root_ready, 1)

            def front_shift(b1):
                xb = x_all[:, bass.ds(b1 * TT, TT), :]
                pool.wait_ge(xn_ready, b1 + 1)
                step.hold()
                pool.tensor_tensor(xb, xb, crow[:].unsqueeze(1).broadcast_to([P, TT, D]), ALU.add).then_inc(x_shifted, 1)

            def post_root(b0):
                w = lnw2
                pool.wait_ge(stats2_ready, b0 + 1)
                step.done(root(w, mv2, LN_EPS))
                step.done(pool.tensor_tensor(w[:, 2, :], w[:, 1, :], w[:, 1, :], ALU.mult))
                step.done(pool.tensor_tensor(w[:, 2, :], w[:, 2, :], mv2[:, :, 1], ALU.mult))
                step.hold()
                step.done(pool.tensor_scalar(w[:, 2, :], w[:, 2, :], RMS_EPS, None, ALU.add))
                step.done(pool.tensor_tensor(w[:, 3, :], w[:, 2, :], nhalf[:], ALU.pow))
                pool.tensor_tensor(w[:, 4, :], w[:, 3, :], w[:, 1, :], ALU.mult).then_inc(root2_ready, 1)
                pool.tensor_scalar(w[:, 5, :], w[:, 1, :], gates[:, 2:3], None, ALU.mult).then_inc(root2_ready, 1)

            def post_skip(b0):
                pool.wait_ge(xt_ready, b0 + 1)
                step.hold()
                pool.tensor_tensor(x_all[:, bass.ds(b0 * TT, TT), :], xp[:], xt[:], ALU.add).then_inc(xp_used, 1)

            def scatter(b0, parts):
                pool.wait_ge(pos_ready, b0 + 1)
                step.hold()
                for j in parts:
                    pool.indirect_dma_start(rows_in, bass.IndirectOffsetOnAxis(ap=pos4[:, j:j + 1], axis=0),
                                            xs[:, j % TT, :], None).then_inc(scattered, 16)

            def batch(b, post, front):
                for s in range(NH):
                    if s == 1 and front:
                        front_root(b + 1)
                    if s == 5 and front:
                        front_shift(b + 1)
                    if s == 6 and post:
                        post_root(b - 1)
                    if s == 9 and post:
                        post_skip(b - 1)
                    if post and s in SCATTER_SLOTS:
                        scatter(b - 1, SCATTER_SLOTS[s])

            pool.memset(zrow[:], 0.0).then_inc(pads_done, 1)
            pool.wait_ge(pads_done, 1)
            pool.dma_start(rows_in[PAD_ROW:ROWS_IN, :], zrow[:]).then_inc(scattered, 16)
            pool.wait_ge(consts_done, CONSTS)
            front_root(0)
            pool.wait_ge(crow_done, 1)
            front_shift(0)
            batch(0, False, True)
            with pool.Fori(1, B - 1) as b:
                step.loop(b - 1, 15)
                batch(b, True, True)
            step.end(B - 2)
            batch(B - 1, True, False)
            batch(B, True, False)
            pool.wait_ge(tables_done, 2)
            for e in range(E):
                pool.indirect_dma_start(rows_in, bass.IndirectOffsetOnAxis(ap=padi[:, e:e + 1], axis=0),
                                        zrow[:], None).then_inc(scattered, 16)
            pool.wait_ge(scattered, 16 * (2 * NT + E + 1))

        @block.scalar
        def _(act):
            act.wait_ge(small_loaded, 64)
            act.activation(gates[:], gates[:], ACT.Tanh).then_inc(gates_done, 1)

            def consume(f, job, bt):
                r = f.bank(job)
                if job in ("xT", "x2T", "qk0", "qk1", "v0", "v1"):
                    f.wait_ready(act, job, bt)
                if job == "xT":
                    act.copy(xnT[:].rearrange("p c s -> p (c s)"), r[:]).then_inc(f.taken_of(job), 1)
                if job == "x2T":
                    act.mul(x2T[:, 0, :], r[:, 0:S], ns[:, 0:1])
                    act.mul(x2T[:, 1, :], r[:, S:2 * S], ns[:, 1:2]).then_inc(f.taken_of(job), 1)
                if job in ("qk0", "qk1"):
                    c = int(job[2])
                    if later(bt):
                        act.wait_ge(qz_ready, bt * NH - 8 + 8 * c)
                        act.wait_ge(scores_ready, bt * NH - 8 + 8 * c)
                    act.activation(qT[:, c, :], r[:, 0:S], ACT.Identity, bias=bqk[:, 0, c:c + 1])
                    act.activation(kT[:, c, :], r[:, S:2 * S], ACT.Identity,
                                   bias=bqk[:, 1, c:c + 1]).then_inc(f.taken_of(job), 1)
                if job in ("v0", "v1"):
                    c = int(job[1])
                    if later(bt):
                        act.wait_ge(out_ready, bt * G0 - 2 + 2 * c)
                    else:
                        act.wait_ge(zeroed, 3)
                    act.copy(V[:, :, 8 * c:8 * c + 8, 0:HD0],
                             r[:, 0:TT * P].rearrange("p (t h d) -> p t h d", t=TT, h=8)).then_inc(f.taken_of(job), 1)

            act.wait_ge(w_loaded, 96)
            for job in ("xT", "qk0", "v0"):
                consume(fam["proj"], job, 0)

            def batch(b, post, front, heads=True):
                for s in range(NH):
                    H = b * NH + s
                    if heads:
                        if later(b) and s == 0:
                            act.wait_ge(rinv_ready, b * 2 - 1)
                        if later(b) and s == 8:
                            act.wait_ge(rinv_ready, b * 2)
                        act.wait_ge(nmax_ready, H + 1)
                        for t, (c0, c1) in enumerate(((0, P), (P, 3 * P))):
                            ins = act.activation(prob[:, s % 2, c0:c1], S_BANK[s % 2][:, c0:c1], ACT.Exp,
                                                 bias=nmax[:, s % 4, t:t + 1], accum_out=den[:, t, s:s + 1])
                        ins.then_inc(probs_ready, 1)
                    for f, job, bt in due(SCHED_A, s, b, post, heads, front):
                        consume(fam[f], job, bt)
                    hp = (s - 3) % NH
                    if hp % G0 == G0 - 1 and (s >= 3 and heads or s < 3 and later(b)):
                        g = hp // G0
                        act.wait_ge(out_ready, b * G0 + (g if s >= 3 else g - G0) + 1)
                        if later(b) and s >= 3:
                            fam["post"].wait_taken(act, "bc1", b - 1)
                        act.copy(oT[:, g, :], O_BANK[g % 2][:, 0:S]).then_inc(out_taken, 1)

            batch(0, False, True)
            with act.Fori(1, B - 1) as b:
                batch(b, True, True)
            batch(B - 1, True, False)
            batch(B, True, False, heads=False)
            act.wait_ge(mixes_done, 1)
            act.activation(gap[:], gap[:], ACT.Exp).then_inc(mixes_done, 1)

        @block.vector
        def _(dve):
            step = Steps(dve, vec_step)
            dve.memset(wo[:], 0.0).then_inc(zeroed, 1)
            dve.memset(bvs[:], 0.0).then_inc(zeroed, 1)
            dve.memset(V[:], 0.0).then_inc(zeroed, 1)
            dve.memset(credit[:, 0:1], 0.0).then_inc(fam["proj"].taken[0], 1)
            dve.memset(credit[:, 2:3], 0.0).then_inc(xp_used, 1)

            def stats(xb, st_, mv_):
                for t in range(TT):
                    ins = dve.bn_stats(st_[:, t, :], xb(t))
                step.done(ins)
                step.hold()
                for t in range(TT):
                    ins = dve.bn_aggr(mv_[:, t, :], st_[:, t, :])
                return ins

            def tile_of(b1):
                return lambda t: x_all[:, bass.ds(b1 * TT + t, 1), :].rearrange("p o d -> p (o d)")

            def normalise(b1):
                dve.wait_ge(root_ready, b1 + 1)
                if later(b1):
                    fam["proj"].wait_ready(dve, "xT", b1 - 1)
                for t in range(TT):
                    ins = dve.tensor_scalar(xn[:, t, :], tile_of(b1)(t), mv[:, t, 0:1], lnw[:, 1, t:t + 1],
                                            ALU.subtract, ALU.mult)
                ins.then_inc(xn_ready, 1)

            def expert_rows(b0):
                dve.wait_ge(root2_ready, 2 * b0 + 2)
                dve.wait_ge(scattered, b0 * (32 * TT) + 16)
                for t in range(TT):
                    ins = dve.tensor_scalar(xs[:, t, :], xp[:, t, :], mv2[:, t, 0:1], lnw2[:, 4, t:t + 1],
                                            ALU.subtract, ALU.mult)
                ins.then_inc(xs_ready, 1)
                dve.wait_ge(xp_used, b0 + 1)
                for t in range(TT):
                    ins = dve.tensor_scalar(xt[:, t, :], xp[:, t, :], mv2[:, t, 0:1], lnw2[:, 5, t:t + 1],
                                            ALU.subtract, ALU.mult)
                ins.then_inc(xt_ready, 1)

            def masked_q(h, b):
                if h % 8 == 0:
                    fam["proj"].wait_taken(dve, f"qk{h // 8}", b)
                dve.tensor_scalar(qz[:, h % 4, :], qT[:, h // 8, :], head_mask[:, h % 8:h % 8 + 1], None,
                                  ALU.mult).then_inc(qz_ready, 1)

            def invert(half):
                h = slice(8 * half, 8 * half + 8)
                dve.reciprocal(rinv[:, :, h], den[:, :, h]).then_inc(rinv_ready, 1)

            def first_of(src, m, one):
                w = rw[:, 0, :].rearrange("p (t e) -> p t e", e=E)
                step.done(dve.tensor_reduce(m, src, AX.X, ALU.max))
                step.done(dve.tensor_tensor(w, src, m.unsqueeze(2).broadcast_to([P, TT, E]), ALU.is_equal))
                step.done(dve.tensor_tensor(w, w, rev[:], ALU.mult))
                step.done(dve.tensor_reduce(r1[:, 3, :], w, AX.X, ALU.max))
                step.done(dve.tensor_tensor(one, rev[:], r1[:, 3, :].unsqueeze(2).broadcast_to([P, TT, E]), ALU.is_equal))

            def te(a):
                return a.rearrange("p (t e) -> p t e", e=E)

            def consume(f, job, bt):
                r = f.bank(job)
                if job in ("rT", "bc0", "bc1", "wo", "rt", "rank"):
                    f.wait_ready(dve, job, bt)
                if job == "rT":
                    dve.tensor_copy(rT[:], r[0:NH, 0:S]).then_inc(f.taken_of(job), 1)
                if job in ("bc0", "bc1"):
                    j = int(job[2])
                    dve.wait_ge(out_taken, bt * G0 + G0)
                    dve.tensor_tensor(oTn[:, 2 * j:2 * j + 2, :], oT[:, 2 * j:2 * j + 2, :],
                                      r[:].rearrange("p (g s) -> p g s", g=2), ALU.mult).then_inc(f.taken_of(job), 1)
                if job == "wo":
                    dve.wait_ge(x_shifted, bt + 1)
                    dve.wait_ge(xp_used, bt + 1)
                    dve.scalar_tensor_tensor(out=xp[:], in0=r[:].rearrange("p (t d) -> p t d", t=TT), scalar=gates[:, 0:1],
                                             in1=x_all[:, bass.ds(bt * TT, TT), :], op0=ALU.mult,
                                             op1=ALU.add).then_inc(f.taken_of(job), 1)
                    f.wait_taken(dve, "wo", bt)
                    stats(lambda t: xp[:, t, :], st2, mv2).then_inc(stats2_ready, 1)
                if job == "rt":
                    dve.tensor_copy(lg[:].rearrange("p t e -> p (t e)"), r[:, 0:TT * E]).then_inc(f.taken_of(job), 1)
                    f.wait_taken(dve, "rt", bt)
                    first_of(lg[:], r1[:, 0, :], te(oh[:, 0, :]))
                    l2 = te(rw[:, 1, :])
                    step.done(dve.scalar_tensor_tensor(out=l2, in0=te(oh[:, 0, :]), scalar=LOWER, in1=lg[:],
                                                       op0=ALU.mult, op1=ALU.add))
                    first_of(l2, r1[:, 1, :], te(oh[:, 1, :]))
                    dve.tensor_tensor(hot[:], oh[:, 0, :], oh[:, 1, :], ALU.add).then_inc(hot_ready, 1)
                    dve.tensor_tensor(gap[:, bass.ds(bt * TT, TT)], r1[:, 1, :], r1[:, 0, :], ALU.subtract)
                if job == "rank":
                    rk = rw[:, 2, :]
                    step.done(dve.tensor_tensor(te(rk), te(r[:, 0:TT * E]), base[:].unsqueeze(1).broadcast_to([P, TT, E]),
                                                ALU.add))
                    dve.tensor_tensor(base[:], base[:], r[:, TT * E:TT * E + E], ALU.add).then_inc(f.taken_of(job), 1)
                    for c in range(2):
                        ins = dve.tensor_tensor(rw[:, 3 + c, :], oh[:, c, :], rk, ALU.mult)
                    step.done(ins)
                    for c in range(2):
                        ins = dve.tensor_reduce(posf[:, c, :], te(rw[:, 3 + c, :]), AX.X, ALU.add)
                    step.done(ins)
                    dve.wait_ge(scattered, bt * (32 * TT) + 16)
                    dve.tensor_copy(pos_all[:, :, bass.ds(bt * TT, TT)], posf[:])
                    dve.tensor_copy(pos4[:], posf[:].rearrange("p c t -> p (c t)")).then_inc(pos_ready, 1)

            dve.wait_ge(wo_loaded, 16 * 2 * G0)
            dve.wait_ge(zeroed, 2)
            for g in range(G0):
                ins = dve.tensor_copy(bvb[:, g, :], columns(bvs[:, g:g + 1], P))
            ins.then_inc(bvb_done, 1)
            dve.wait_ge(x0_loaded, 16)
            stats(tile_of(0), st, mv).then_inc(stats_ready, 1)
            normalise(0)
            dve.wait_ge(crow_ready, 1)
            dve.wait_ge(gates_done, 1)
            step.done(dve.tensor_tensor(crow[:], crow[:], fam["post"].bank("rT")[:, 0:D], ALU.add))
            dve.tensor_scalar(crow[:], crow[:], gates[:, 0:1], None, ALU.mult).then_inc(crow_done, 1)
            dve.memset(credit[:, 1:2], 0.0).then_inc(fam["post"].taken[0], 1)
            dve.wait_ge(consts_done, CONSTS)
            dve.wait_ge(tables_done, 1)

            def batch(b, post, front, heads=True):
                for s in range(NH):
                    H = b * NH + s
                    if s >= 2 and heads or s < 2 and later(b):
                        dve.wait_ge(pT_ready, H - 1)
                        hb = (s - 2) % NPT
                        if later(b) or s - 2 >= NPT:
                            dve.wait_ge(out_ready, b * G0 + (s - 2) // G0 - 1)
                        dve.tensor_copy(pT[:, hb, :], T_BANK[s % 2][:, 0:384]).then_inc(pT_taken, 1)
                    if heads:
                        dve.wait_ge(scores_ready, H + 1)
                        sc = S_BANK[s % 2]
                        dve.tensor_reduce(nmax[:, s % 4, 0:1], sc[:, 0:P], AX.X, ALU.max, negate=True)
                        dve.tensor_reduce(nmax[:, s % 4, 1:2], sc[:, P:3 * P], AX.X, ALU.max,
                                          negate=True).then_inc(nmax_ready, 1)
                    if s == 1 and later(b):
                        dve.wait_ge(probs_ready, b * NH)
                        invert(1)
                    if s == 9 and heads:
                        dve.wait_ge(probs_ready, b * NH + 8)
                        invert(0)
                    if s == 1 and front:
                        dve.wait_ge(root_ready, b + 1)
                        step.hold()
                        stats(tile_of(b + 1), st, mv).then_inc(stats_ready, 1)
                    if s == 4 and front:
                        normalise(b + 1)
                    if s == 8 and post:
                        expert_rows(b - 1)
                    if heads and s < NH - 2:
                        masked_q(s + 2, b)
                    if front and s >= NH - 2:
                        masked_q(s + 2 - NH, b + 1)
                    for f, job, bt in due(SCHED_A, s, b, post, heads, front):
                        consume(fam[f], job, bt)

            dve.wait_ge(x_loaded, 16)
            masked_q(0, 0)
            masked_q(1, 0)
            batch(0, False, True)
            with dve.Fori(1, B - 1) as b:
                step.loop(b - 1, 19)
                batch(b, True, True)
            step.end(B - 2)
            batch(B - 1, True, False)
            batch(B, True, False, heads=False)

            dve.wait_ge(tables_done, 1)
            cnt, tiles, ends = small[:, 40:48], small[:, 48:56], small[:, 56:64]
            ends2 = small[:, 64:72]
            nxt, rof = small[:, 72:112], small[:, 112:152]
            for e in range(E):
                ins = dve.tensor_scalar(cnt[:, e:e + 1], base[:, e:e + 1], float(CAP * e), None, ALU.subtract)
            step.done(ins)
            t16 = tab[:, 0:E * 16].rearrange("p (e j) -> p e j", j=16)
            step.done(dve.tensor_tensor(t16, cnt.unsqueeze(2).broadcast_to([P, E, 16]), t16, ALU.is_gt))
            step.done(dve.tensor_reduce(tiles, t16, AX.X, ALU.add))
            step.done(dve.tensor_tensor(padf[:], padf[:], base[:], ALU.add))
            dve.tensor_copy(padi[:], padf[:]).then_inc(tables_done, 1)
            src, dst = tiles, ends
            for sh in (1, 2, 4):
                step.done(dve.tensor_copy(dst[:, 0:sh], src[:, 0:sh]))
                step.done(dve.tensor_tensor(dst[:, sh:E], src[:, sh:E], src[:, 0:E - sh], ALU.add))
                src, dst = dst, (ends2 if dst is ends else ends)
            past = tab2[:].rearrange("p (i e) -> p i e", e=E)
            step.done(dve.tensor_tensor(past, past, src.unsqueeze(1).broadcast_to([P, 40, E]), ALU.is_ge))
            step.done(dve.tensor_reduce(nxt, past, AX.X, ALU.add))
            pt = tab[:].rearrange("p (i e) -> p i e", e=E)
            step.done(dve.tensor_tensor(pt, past, tiles.unsqueeze(1).broadcast_to([P, 40, E]), ALU.mult))
            step.done(dve.tensor_reduce(rof, pt, AX.X, ALU.add))
            step.done(dve.scalar_tensor_tensor(out=rof, in0=rof, scalar=-float(P), in1=small[:, 0:40],
                                               op0=ALU.mult, op1=ALU.add))
            step.done(dve.scalar_tensor_tensor(out=rof, in0=nxt, scalar=float(CAP), in1=rof,
                                               op0=ALU.mult, op1=ALU.add))
            step.done(dve.tensor_scalar(rof, rof, float(PAD_ROW), None, ALU.min))
            step.done(dve.tensor_scalar(nxt, nxt, float(E - 1), None, ALU.min))
            dve.tensor_copy(row_tab[:], rof[0:1, :])
            dve.tensor_copy(exp_tab[:], nxt[0:1, :]).then_inc(mixes_done, 1)
            move = small[:, 40:48]
            moved = tab2[:, 0:2 * NT * E].rearrange("p (i e) -> p i e", e=E)
            all_rows = pos_all[:].rearrange("p c t -> p (c t)")
            dve.tensor_copy(moved[:, :, E - 1], all_rows)
            step.done(dve.tensor_scalar(move, tiles, float(P), float(CAP), ALU.mult, ALU.subtract))
            for e in range(1, E):
                ins = dve.tensor_scalar(moved[:, :, e - 1], moved[:, :, E - 1], float(CAP * e), move[:, e - 1:e],
                                        ALU.is_ge, ALU.mult)
            step.done(ins)
            step.done(dve.tensor_reduce(small[:, 112:144], moved, AX.X, ALU.add))
            step.done(dve.tensor_copy(all_rows, small[:, 112:144]))
            dve.wait_ge(mixes_done, 2)
            step.done(dve.tensor_scalar(mix[:, 0, :], gap[:], 1.0, None, ALU.add))
            step.done(dve.reciprocal(mix[:, 0, :], mix[:, 0, :]))
            step.done(dve.tensor_scalar(mix[:, 0, :], mix[:, 0, :], gates[:, 2:3], None, ALU.mult))
            step.done(dve.tensor_tensor(mix[:, 1, :], mix[:, 0, :], gap[:], ALU.mult))

        @block.tensor
        def _(pe):
            mm = pe.matmul

            def fill(f, job, bt):
                r = f.bank(job)
                f.wait_free(pe, job, bt)
                if job == "xT":
                    pe.wait_ge(xn_ready, bt + 1)
                    for c in range(DC):
                        for t in range(TT):
                            o = c * S + t * P
                            ins = pe.transpose(r[:, o:o + P], xn[:, t, c * P:c * P + P], ident[:])
                if job in ("qk0", "qk1"):
                    c = int(job[2])
                    f.wait_other(pe, job, "xT", bt)
                    pe.wait_ge(ctx_loaded, bt * 16 + 16)
                    for j, (w, a) in enumerate(((wq, xnT), (wk, cT))):
                        for d in range(DC):
                            ins = mm(r[:, j * S:j * S + S], w[:, d, c * P:c * P + P], a[:, d, :],
                                     start=d == 0, stop=d == DC - 1)
                if job in ("v0", "v1"):
                    c = int(job[1])
                    pe.wait_ge(ctx_loaded, bt * 16 + 16)
                    for t in range(TT):
                        for d in range(DC):
                            ins = mm(r[:, t * P:t * P + P], cT[:, d, t * P:t * P + P], wv[:, d, c * P:c * P + P],
                                     start=d == 0, stop=d == DC - 1)
                if job == "rT":
                    pe.wait_ge(rinv_ready, bt * 2 + 2)
                    for t in range(TT):
                        ins = mm(r[0:NH, t * P:t * P + P], rinv[:, t, :], ident[:], start=True, stop=True)
                if job in ("bc0", "bc1"):
                    j = int(job[2])
                    f.wait_other(pe, job, "rT", bt)
                    for i in range(2):
                        ins = mm(r[:, i * S:i * S + S], sel[:, 2 * j + i, :], rT[:], start=True, stop=True)
                if job == "wo":
                    f.wait_other(pe, job, "bc1", bt)
                    for t in range(TT):
                        for g in range(G0):
                            ins = mm(r[:, t * D:t * D + D], oTn[:, g, t * P:t * P + P], wo[:, g, :],
                                     start=g == 0, stop=g == G0 - 1)
                if job == "x2T":
                    pe.wait_ge(xs_ready, bt + 1)
                    for c in range(DC):
                        for t in range(TT):
                            o = c * S + t * P
                            ins = pe.transpose(r[:, o:o + P], xs[:, t, c * P:c * P + P], ident[:])
                if job == "rt":
                    f.wait_other(pe, job, "x2T", bt)
                    for t in range(TT):
                        for c in range(DC):
                            ins = mm(r[:, t * E:t * E + E], x2T[:, c, t * P:t * P + P], wr[:, c, :],
                                     start=c == 0, stop=c == DC - 1)
                if job == "rank":
                    pe.wait_ge(hot_ready, bt + 1)
                    mm(r[:, 0:E], tri[:], hot[:, 0:E], start=True, stop=True)
                    mm(r[:, E:2 * E], tri[:], hot[:, E:2 * E], start=True, stop=False)
                    mm(r[:, E:2 * E], ones[:], hot[:, 0:E], start=False, stop=True)
                    mm(r[:, 2 * E:3 * E], ones[:], hot[:, 0:E], start=True, stop=False)
                    ins = mm(r[:, 2 * E:3 * E], ones[:], hot[:, E:2 * E], start=False, stop=True)
                ins.then_inc(f.ready_of(job), 1)

            pe.wait_ge(consts_done, CONSTS)
            pe.wait_ge(w_loaded, 96)
            pe.wait_ge(bvb_done, 1)
            for g in range(G0):
                ins = mm(fam["post"].bank("rT")[:, 0:D], bvb[:, g, :], wo[:, g, :], start=g == 0, stop=g == G0 - 1)
            ins.then_inc(crow_ready, 1)
            for job in ("xT", "qk0", "v0"):
                fill(fam["proj"], job, 0)

            def turn(b, s):
                H = b * NH + s
                pe.wait_ge(probs_ready, H - 1)
                if later(b) or s >= 4:
                    pe.wait_ge(pT_taken, H - 3)
                o, p = T_BANK[s % 2], prob[:, s % 2, :]
                pe.transpose(o[:, 0:P], p[:, 0:P], ident[:])
                pe.transpose(o[:, P:2 * P], p[:, P:2 * P], ident[:])
                pe.transpose(o[:, 2 * P:3 * P], p[:, 2 * P:3 * P], ident[:]).then_inc(pT_ready, 1)

            def scores(b, s):
                H = b * NH + s
                c = s // 8
                if s % 8 == 0:
                    fam["proj"].wait_taken(pe, f"qk{c}", b)
                pe.wait_ge(qz_ready, H + 1)
                q, k, o = qz[:, s % 4, :], kT[:, c, :], S_BANK[s % 2]
                mm(o[:, 0:P], q[:, 0:P], k[:, 0:P], start=True, stop=False)
                mm(o[:, CHUNK:P], mrow[:], mneg[:], start=False, stop=True)
                mm(o[:, P:3 * P], q[:, P:2 * P], k, start=True, stop=False)
                mm(o[:, 3 * P - CHUNK:3 * P], mrow[:], mneg[:], start=False, stop=True).then_inc(scores_ready, 1)

            def values(b, s):
                hp = (s - 3) % NH
                g = hp // G0
                G = b * G0 + (g if s >= 3 else g - G0)
                pe.wait_ge(pT_taken, b * NH + s - 2)
                if later(b) or g >= 2:
                    pe.wait_ge(out_taken, G - 1)
                if g % 2 == 0:
                    fam["proj"].wait_taken(pe, f"v{g // 2}", b)
                o = O_BANK[g % 2]
                for kt in range(TT):
                    for j in range(G0):
                        h = g * G0 + j
                        pj = pT[:, h % NPT, :]
                        ins = mm(o[SLOT0 * j:SLOT0 * (j + 1), kt * P:S], V[:, kt, h, :],
                                 pj[:, 0:S] if kt == 0 else pj[:, S:S + P], start=kt == 0, stop=kt == 1)
                ins.then_inc(out_ready, 1)

            def batch(b, post, front, heads=True):
                for s in range(NH):
                    if s >= 2 and heads or s < 2 and later(b):
                        turn(b, s)
                    if heads:
                        scores(b, s)
                    for f, job, bt in due(SCHED_A, s, b, post, heads, front):
                        fill(fam[f], job, bt)
                    if (s - 3) % NH % G0 == G0 - 1 and (s >= 3 and heads or s < 3 and later(b)):
                        values(b, s)

            batch(0, False, True)
            with pe.Fori(1, B - 1) as b:
                batch(b, True, True)
            batch(B - 1, True, False)
            batch(B, True, False, heads=False)


def later(b):
    return not isinstance(b, int) or b > 0


def phase_b(nc, v, ctx, w1, w1_loaded):
    bank, ident, ns, row_tab, exp_tab = (v[k] for k in ("bank", "ident", "ns", "row_tab", "exp_tab"))
    w_up, w_dn, rows_in, rows_out = (v[k] for k in ("w_up", "w_dn", "rows_in", "rows_out"))
    sb = lambda name, shape, dt=F32: ctx.enter_context(nc.sbuf_tensor(name, shape, dt))
    sem = lambda name: ctx.enter_context(nc.semaphore(name))
    xg = sb("xg", [P, 2, D])
    xgT = sb("xgT", [P, 2, DC * P])
    sg = sb("sg", [P, 2, HID])
    hh = sb("hh", [P, 2, HID])
    hT = sb("hT", [P, 2, HID])
    yy = sb("yy", [P, 2, D])
    loaded = [sem("rows0_loaded"), sem("rows1_loaded")]
    stored = [sem("rows0_stored"), sem("rows1_stored")]
    xT_ready, xT_taken, up_ready, silu_ready, h_ready = (sem(n) for n in (
        "moe_xT_ready", "moe_xT_taken", "moe_up_ready", "moe_silu_ready", "moe_h_ready"))
    hT_ready, hT_taken, y_ready, y_taken = (sem(n) for n in ("moe_hT_ready", "moe_hT_taken", "moe_y_ready", "moe_y_taken"))
    all_sems = (xT_ready, xT_taken, up_ready, silu_ready, h_ready, hT_ready, hT_taken, y_ready, y_taken)
    X_BANK, U_BANK, GATE_BANK, HT_BANK, Y_BANK = bank[0], bank[1:3], bank[3:5], bank[5:7], bank[7]
    LOOPED = TILES - 3
    assert LOOPED % 2 == 0

    def tiles(eng, slot):
        with eng.Fori(0, LOOPED // 2) as t:
            slot(t * 2, 0, t)
            slot(t * 2 + 1, 1, t)
        for i in range(LOOPED, TILES):
            slot(i, i % 2, i // 2)

    def exists(i):
        return not isinstance(i, int) or i < TILES

    block = ctx.enter_context(nc.Block())

    @block.sync
    def _(sp):
        def load(i, u, t):
            row = sp.value_load(row_tab[0:1, bass.ds(i, 1)], min_val=0, max_val=PAD_ROW)
            sp.dma_start(xg[:, u, :], rows_in[bass.ds(row, P), :]).then_inc(loaded[u], 16)

        load(0, 0, 0)
        load(1, 1, 0)
        for dst, src in w1:
            sp.dma_start(dst, src).then_inc(w1_loaded, 16)

        def slot(i, u, t):
            if exists(i + 2):
                sp.wait_ge(xT_ready, i + 1 + 2)
                load(i + 2, u, t + 1)
            sp.wait_ge(y_taken, i + 1 + 2)
            sp.dma_start(rows_out[bass.ds(i * P, P), :], yy[:, u, :]).then_inc(stored[u], 16)

        tiles(sp, slot)
        for u in range(2):
            sp.wait_ge(stored[u], 16 * (1 + (TILES + 1 - u) // 2))

    @block.scalar
    def _(act):
        for k in (xT_ready, xT_taken, up_ready, silu_ready, h_ready, hT_ready, hT_taken, y_ready, y_taken):
            act.sem_inc(k, 2)
        for k in stored:
            act.sem_inc(k, 16)

        def take_x(i, u):
            act.wait_ge(xT_ready, i + 1 + 2)
            for c in range(DC):
                ins = act.mul(xgT[:, u, c * P:c * P + P], X_BANK[:, c * P:c * P + P], ns[:, c:c + 1])
            ins.then_inc(xT_taken, 1)

        def silu(i, u):
            act.wait_ge(up_ready, i + 1 + 2)
            act.wait_ge(h_ready, i - 1 + 2)
            act.activation(sg[:, u, :], GATE_BANK[u][:], ACT.Silu).then_inc(silu_ready, 1)

        take_x(0, 0)
        silu(0, 0)
        take_x(1, 1)

        def slot(i, u, t):
            if exists(i + 1):
                silu(i + 1, 1 - u)
            if exists(i + 2):
                take_x(i + 2, u)
            act.wait_ge(y_ready, i + 1 + 2)
            act.wait_ge(stored[u], t * 16 + 16)
            act.copy(yy[:, u, :], Y_BANK[:, 0:D]).then_inc(y_taken, 1)

        tiles(act, slot)

    @block.vector
    def _(dve):
        def gated(i, u):
            dve.wait_ge(silu_ready, i + 1 + 2)
            dve.tensor_tensor(hh[:, u, :], U_BANK[u][:], sg[:, u, :], ALU.mult).then_inc(h_ready, 1)

        gated(0, 0)

        def slot(i, u, t):
            dve.wait_ge(hT_ready, i + 1 + 2)
            dve.wait_ge(y_ready, i - 1 + 2)
            dve.tensor_copy(hT[:, u, :], HT_BANK[u][:]).then_inc(hT_taken, 1)
            if exists(i + 1):
                gated(i + 1, 1 - u)

        tiles(dve, slot)

    @block.tensor
    def _(pe):
        def turn_x(i, u, t):
            pe.wait_ge(loaded[u], t * 16 + 16)
            pe.wait_ge(xT_taken, i + 2)
            for c in range(DC):
                ins = pe.transpose(X_BANK[:, c * P:c * P + P], xg[:, u, c * P:c * P + P], ident[:])
            ins.then_inc(xT_ready, 1)

        def up(i, u):
            e = pe.value_load(exp_tab[0:1, bass.ds(i, 1)], min_val=0, max_val=E - 1)
            pe.wait_ge(xT_taken, i + 1 + 2)
            pe.wait_ge(h_ready, i - 1 + 2)
            for half, o in ((1, GATE_BANK[u]), (0, U_BANK[u])):
                for c in range(DC):
                    ins = pe.matmul(o[:], xgT[:, u, c * P:c * P + P],
                                    w_up[:, bass.ds(e * (DC * 2 * HID) + (c * 2 * HID + half * HID), HID)],
                                    start=c == 0, stop=c == DC - 1)
            ins.then_inc(up_ready, 1)

        def down(i, u):
            e = pe.value_load(exp_tab[0:1, bass.ds(i, 1)], min_val=0, max_val=E - 1)
            pe.wait_ge(hT_taken, i + 1 + 2)
            pe.wait_ge(y_taken, i + 2)
            for c in range(HC):
                ins = pe.matmul(Y_BANK[:, 0:D], hT[:, u, c * P:c * P + P],
                                w_dn[:, bass.ds(e * (HC * D) + c * D, D)], start=c == 0, stop=c == HC - 1)
            ins.then_inc(y_ready, 1)

        pe.wait_ge(v["moe_loaded"], 16 * 2 * E)
        pe.wait_ge(y_taken, 2)
        turn_x(0, 0, 0)
        up(0, 0)
        turn_x(1, 1, 0)

        def slot(i, u, t):
            pe.wait_ge(h_ready, i + 1 + 2)
            pe.wait_ge(hT_taken, i - 1 + 2)
            for c in range(HC):
                ins = pe.transpose(HT_BANK[u][:, c * P:c * P + P], hh[:, u, c * P:c * P + P], ident[:])
            ins.then_inc(hT_ready, 1)
            if exists(i + 1):
                up(i + 1, 1 - u)
            if exists(i + 2):
                turn_x(i + 2, u, t + 1)
            down(i, u)

        tiles(pe, slot)


def phase_c(nc, v, ctx, w, w1_loaded):
    x_all, bank, ident, gates, nhalf = (v[k] for k in ("x_all", "bank", "ident", "gates", "nhalf"))
    mix, pos_all, rows_out, ctxT, out = (v[k] for k in ("mix", "pos_all", "rows_out", "ctxT", "out"))
    wq, wkv, wo, wi, wd, lB, lA, gw, gb, crow, crow3, bi = (w[k] for k in (
        "wq", "wkv", "wo", "wi", "wd", "lB", "lA", "gw", "gb", "crow1", "crow3", "bi"))
    sb = lambda name, shape, dt=F32: ctx.enter_context(nc.sbuf_tensor(name, shape, dt))
    sem = lambda name: ctx.enter_context(nc.semaphore(name))
    spaces = [[v["w_up"], 0, E * DC * 2 * HID], [v["w_dn"], 0, E * HC * D]]

    def work(*dims):
        n = int(np.prod(dims))
        space = next(x for x in spaces if x[1] + n <= x[2])
        space[1] += n
        a = space[0][:, space[1] - n:space[1]]
        if len(dims) == 2:
            return a.rearrange("p (a b) -> p a b", a=dims[0])
        return a.rearrange("p (a b c) -> p a b c", a=dims[0], b=dims[1]) if len(dims) == 3 else a

    NP1 = NH // G1
    NPT1 = 4
    oT, oTn, pT, hT = work(NP1, S), work(NP1, S), work(NPT1, 2 * S), work(FC, S)
    prob, qk, V, yg = work(2, 2 * S), work(2, 2 * S), work(4, TT, P), work(2, TT, D)
    xn, xnT, cT, x3n, x3T = work(TT, D), work(DC, S), work(DC, S), work(TT, D), work(DC, S)
    am, amT, t2, xq, xp, ob = work(TT, 2, P), work(2, S), work(2, S), work(TT, D), work(TT, D), work(TT, D)
    biB = work(FC, P)
    nbi = sb("nbi", [P, FC])
    sel = sb("sel1", [NH, NP1, P])
    nmax = sb("nmax1", [P, 4, TT])
    den = sb("den1", [P, TT, NH])
    rinv = sb("rinv1", [P, TT, NH])
    rT = sb("rT1", [NH, S])
    st = sb("st1", [P, TT, 6])
    mv = sb("mv1", [P, TT, 2])
    st2 = sb("st12", [P, TT, 6])
    mv2 = sb("mv12", [P, TT, 2])
    lnw = sb("lnw1", [P, 2, TT])
    lnw2 = sb("lnw12", [P, 2, TT])
    rev = sb("rev1", [P, TT, E])
    lg = sb("lg1", [P, TT, E])
    pr = sb("pr1", [P, TT, E])
    rw = sb("rw1", [P, 2, TT * E])
    r1 = sb("r11", [P, 6, TT])
    oh = sb("oh1", [P, 2, TT * E])
    idx4 = sb("idx4", [P, 2, TT], U32)

    ctx_loaded, gathered = sem("ctx_loaded1"), sem("gathered")
    consts_done, weights_done = sem("consts_done1"), sem("weights_done")
    biB_done, crow3_ready = sem("biB_done"), sem("crow3_ready")
    scores_ready, nmax_ready, probs_ready = sem("scores_ready1"), sem("nmax_ready1"), sem("probs_ready1")
    pT_ready, pT_taken = sem("pT_ready1"), sem("pT_taken1")
    out_ready, out_taken, rinv_ready = sem("out_ready1"), sem("out_taken1"), sem("rinv_ready1")
    xq_ready, stats_ready, root_ready, xn_ready, x_shifted = (sem(n) for n in (
        "xq_ready", "stats_ready1", "root_ready1", "xn_ready1", "x_shifted1"))
    stats2_ready, root2_ready, x3_ready = sem("stats2_ready1"), sem("root2_ready1"), sem("x3_ready")
    shifted_ready, exp_ready, am_ready, relu_ready = (sem(n) for n in (
        "logits_shifted", "logits_exp", "am_ready", "relu_ready"))
    final_ready, final_stored = sem("final_ready"), sem("final_stored")
    vec_step, pool_step = sem("vec_step_c"), sem("pool_step_c")
    S_BANK, T_BANK, O_BANK = bank[0:2], bank[2:4], bank[4]
    fam = {"proj": Family(PROJ_C, [bank[5]], [sem("proj_ready1")], [sem("proj_taken1")]),
           "post": Family(POST_C, bank[6:8], [sem("post0_ready1"), sem("post1_ready1")],
                          [sem("post0_taken1"), sem("post1_taken1")])}
    W1_LOADS = 16 * 12
    block = ctx.enter_context(nc.Block())

    @block.sync
    def _(sp):
        cv = ctxT.rearrange("b (c p) s -> b p c s", p=P)
        ov = out.rearrange("b (t p) d -> b p t d", p=P)

        def context(b):
            sp.dma_start(cT, cv[bass.ds(b, 1)].rearrange("o p c s -> (o p) c s")).then_inc(ctx_loaded, 16)

        def next_context(b):
            fam["proj"].wait_ready(sp, "v7", b)
            context(b + 1)

        def store(b):
            sp.wait_ge(final_ready, b + 1)
            sp.dma_start(ov[bass.ds(b, 1)].rearrange("o p t d -> (o p) t d"), ob).then_inc(final_stored, 16)

        context(0)
        next_context(0)
        with sp.Fori(1, B - 1) as b:
            next_context(b)
            store(b - 1)
        store(B - 2)
        store(B - 1)
        sp.wait_ge(final_stored, 16 * (B + 1))

    @block.gpsimd
    def _(pool):
        step = Steps(pool, pool_step)

        def gather(b1):
            if later(b1):
                pool.wait_ge(xq_ready, b1)
                step.hold()
            step.done(pool.tensor_copy(idx4[:], pos_all[:, :, bass.ds(b1 * TT, TT)]))
            step.hold()
            for c in range(2):
                for t in range(TT):
                    pool.indirect_dma_start(yg[:, c, t, :], None, rows_out,
                                            bass.IndirectOffsetOnAxis(ap=idx4[:, c, t:t + 1], axis=0)).then_inc(gathered, 16)

        def root(w, m, ready):
            step.hold()
            step.done(pool.tensor_scalar(w[:, 0, :], m[:, :, 1], LN_EPS, None, ALU.add))
            pool.tensor_tensor(w[:, 1, :], w[:, 0, :], nhalf[:], ALU.pow).then_inc(ready, 1)

        def front_root(b1):
            pool.wait_ge(stats_ready, b1 + 1)
            root(lnw, mv, root_ready)

        def front_shift(b1):
            pool.wait_ge(xn_ready, b1 + 1)
            step.hold()
            pool.tensor_tensor(x_all[:, bass.ds(b1 * TT, TT), :], xq,
                               crow[:].unsqueeze(1).broadcast_to([P, TT, D]), ALU.add).then_inc(x_shifted, 1)

        def post_root(b0):
            pool.wait_ge(stats2_ready, b0 + 1)
            root(lnw2, mv2, root2_ready)

        def batch(b, post, front):
            for s in range(NH):
                if s == 0 and front:
                    gather(b + 1)
                if s == 6 and front:
                    front_root(b + 1)
                if s == 7 and post:
                    post_root(b - 1)
                if s == 10 and front:
                    front_shift(b + 1)

        pool.wait_ge(w1_loaded, W1_LOADS)
        gather(0)
        step.done(pool.memset(sel[:], 1.0))
        sv = sel[:].rearrange("h g (j d) -> h g j d", j=G1)
        pool.affine_select(out=sv, in_=sv, compare_op=ALU.is_equal, fill=0.0, base=0,
                           pattern=[[-G1, NP1], [-1, G1], [0, HD1]], channel_multiplier=1).then_inc(consts_done, 1)
        pool.iota(rev[:], pattern=[[0, TT], [-1, E]], base=E, channel_multiplier=0,
                  allow_small_or_imprecise_dtypes=True).then_inc(consts_done, 1)
        front_root(0)
        pool.wait_ge(weights_done, 4)
        front_shift(0)
        batch(0, False, True)
        with pool.Fori(1, B - 1) as b:
            step.loop(b - 1, 8)
            batch(b, True, True)
        step.end(B - 2)
        batch(B - 1, True, False)
        batch(B, True, False)

    @block.scalar
    def _(act):
        act.wait_ge(w1_loaded, W1_LOADS)
        act.mul(wq[:], wq[:], HD1 ** -0.5).then_inc(weights_done, 1)
        act.mul(nbi[:], bi[:], -1.0).then_inc(weights_done, 1)
        act.mul(crow[:], crow[:], gates[:, 1:2]).then_inc(weights_done, 1)
        act.sem_inc(final_stored, 16)
        for f in fam.values():
            for k in f.taken:
                act.sem_inc(k, 1)

        def consume(f, job, bt):
            r = f.bank(job)
            if job[0:2] in ("xT", "x3", "qk", "la", "up") and job != "la":
                f.wait_ready(act, job, bt)
            if job == "xT":
                act.copy(xnT.rearrange("p c s -> p (c s)"), r[:]).then_inc(f.taken_of(job), 1)
            if job == "x3T":
                act.copy(x3T.rearrange("p c s -> p (c s)"), r[:]).then_inc(f.taken_of(job), 1)
            if job == "laT":
                act.copy(amT.rearrange("p c s -> p (c s)"), r[:]).then_inc(f.taken_of(job), 1)
            if job[0:2] == "qk":
                p = int(job[2])
                if p >= 2 or later(bt):
                    act.wait_ge(scores_ready, bt * NH + 2 * p - 2)
                act.copy(qk[:, p % 2, :], r[:]).then_inc(f.taken_of(job), 1)
            if job == "rt":
                act.wait_ge(shifted_ready, bt + 1)
                act.activation(pr[:], lg[:], ACT.Exp).then_inc(exp_ready, 1)
            if job[0:2] == "up":
                c = int(job[2])
                if c >= 2:
                    f.wait_taken(act, f"up{c - 2}", bt)
                act.activation(t2[:, c % 2, :], r[:, S:2 * S], ACT.Relu, bias=bi[:, c:c + 1]).then_inc(relu_ready, 1)

        consume(fam["proj"], "xT", 0)
        consume(fam["proj"], "qk0", 0)

        def batch(b, post, front, heads=True):
            for s in range(NH):
                H = b * NH + s
                if heads:
                    if later(b) and s == 0:
                        act.wait_ge(rinv_ready, b * 2 - 1)
                    if later(b) and s == 8:
                        act.wait_ge(rinv_ready, b * 2)
                    act.wait_ge(nmax_ready, H + 1)
                    for t in range(TT):
                        ins = act.activation(prob[:, s % 2, t * S:t * S + S], S_BANK[s % 2][:, t * S:t * S + S], ACT.Exp,
                                             bias=nmax[:, s % 4, t:t + 1], accum_out=den[:, t, s:s + 1])
                    ins.then_inc(probs_ready, 1)
                for f, job, bt in due(SCHED_C, s, b, post, heads, front):
                    consume(fam[f], job, bt)
                if s % G1 == 0 and (s >= 4 and heads or s < 4 and later(b)):
                    g = (s - 4) % NH // G1
                    act.wait_ge(out_ready, b * NP1 + (s - 4) // G1 + 1)
                    if later(b) and s >= 4:
                        fam["post"].wait_taken(act, "bc0" if g < 2 else "bc1" if g < 4 else "bc3", b - 1)
                    act.copy(oT[:, g, :], O_BANK[:, 0:S]).then_inc(out_taken, 1)

        batch(0, False, True)
        with act.Fori(1, B - 1) as b:
            batch(b, True, True)
        batch(B - 1, True, False)
        batch(B, True, False, heads=False)

    @block.vector
    def _(dve):
        step = Steps(dve, vec_step)
        dve.wait_ge(w1_loaded, W1_LOADS)

        def te(a):
            return a.rearrange("p (t e) -> p t e", e=E)

        def stats(a, st_, mv_):
            for t in range(TT):
                ins = dve.bn_stats(st_[:, t, :], a[:, t, :])
            step.done(ins)
            step.hold()
            for t in range(TT):
                ins = dve.bn_aggr(mv_[:, t, :], st_[:, t, :])
            return ins

        def combine(b1):
            dve.wait_ge(gathered, b1 * (32 * TT) + 32 * TT)
            if later(b1):
                dve.wait_ge(x_shifted, b1)
            for t in range(TT):
                ins = dve.scalar_tensor_tensor(
                    out=xq[:, t, :], in0=yg[:, 0, t, :], scalar=mix[:, 0, bass.ds(b1 * TT + t, 1)],
                    in1=x_all[:, bass.ds(b1 * TT + t, 1), :].rearrange("p o d -> p (o d)"), op0=ALU.mult, op1=ALU.add)
            step.done(ins)
            for t in range(TT):
                ins = dve.scalar_tensor_tensor(
                    out=xq[:, t, :], in0=yg[:, 1, t, :], scalar=mix[:, 1, bass.ds(b1 * TT + t, 1)],
                    in1=xq[:, t, :], op0=ALU.mult, op1=ALU.add)
            ins.then_inc(xq_ready, 1)
            dve.wait_ge(xq_ready, b1 + 1)
            step.hold()
            stats(xq, st, mv).then_inc(stats_ready, 1)

        def normalise(b1):
            dve.wait_ge(root_ready, b1 + 1)
            if later(b1):
                fam["proj"].wait_ready(dve, "xT", b1 - 1)
            for t in range(TT):
                ins = dve.tensor_scalar(xn[:, t, :], xq[:, t, :], mv[:, t, 0:1], lnw[:, 1, t:t + 1],
                                        ALU.subtract, ALU.mult)
            ins.then_inc(xn_ready, 1)

        def normalise3(b0):
            dve.wait_ge(root2_ready, b0 + 1)
            for t in range(TT):
                ins = dve.tensor_scalar(x3n[:, t, :], xp[:, t, :], mv2[:, t, 0:1], lnw2[:, 1, t:t + 1],
                                        ALU.subtract, ALU.mult)
            ins.then_inc(x3_ready, 1)

        def invert(half):
            h = slice(8 * half, 8 * half + 8)
            dve.reciprocal(rinv[:, :, h], den[:, :, h]).then_inc(rinv_ready, 1)

        def first_of(src, m, one):
            a = te(rw[:, 0, :])
            step.done(dve.tensor_reduce(m, src, AX.X, ALU.max))
            step.done(dve.tensor_tensor(a, src, m.unsqueeze(2).broadcast_to([P, TT, E]), ALU.is_equal))
            step.done(dve.tensor_tensor(a, a, rev[:], ALU.mult))
            step.done(dve.tensor_reduce(r1[:, 3, :], a, AX.X, ALU.max))
            step.done(dve.tensor_tensor(one, rev[:], r1[:, 3, :].unsqueeze(2).broadcast_to([P, TT, E]), ALU.is_equal))

        def choose():
            step.done(dve.tensor_reduce(r1[:, 4, :], pr[:], AX.X, ALU.add))
            step.done(dve.reciprocal(r1[:, 4, :], r1[:, 4, :]))
            step.done(dve.tensor_tensor(pr[:], pr[:], r1[:, 4, :].unsqueeze(2).broadcast_to([P, TT, E]), ALU.mult))
            first_of(pr[:], r1[:, 0, :], te(oh[:, 0, :]))
            p2 = te(rw[:, 1, :])
            step.done(dve.scalar_tensor_tensor(out=p2, in0=te(oh[:, 0, :]), scalar=LOWER, in1=pr[:],
                                               op0=ALU.mult, op1=ALU.add))
            first_of(p2, r1[:, 1, :], te(oh[:, 1, :]))
            step.done(dve.tensor_tensor(r1[:, 2, :], r1[:, 0, :], r1[:, 1, :], ALU.add))
            step.done(dve.tensor_scalar(r1[:, 5, :], r1[:, 2, :], gates[:, 3:4], None, ALU.mult))

        def consume(f, job, bt):
            r = f.bank(job)
            taken = f.taken_of(job)
            if job[0] in "vbwr" or job in ("la", "down") or job[0:2] == "up":
                f.wait_ready(dve, job, bt)
            if job[0] == "v":
                p = int(job[1])
                if p >= 4 or later(bt):
                    dve.wait_ge(out_ready, bt * NP1 + p - 3)
                dve.tensor_copy(V[:, p % 4, :, :].rearrange("p t d -> p (t d)"), r[:, 0:TT * P]).then_inc(taken, 1)
            if job == "rT":
                dve.tensor_copy(rT[:], r[0:NH, 0:S]).then_inc(taken, 1)
            if job[0:2] == "bc":
                j = int(job[2])
                dve.wait_ge(out_taken, bt * NP1 + NP1)
                dve.tensor_tensor(oTn[:, 2 * j:2 * j + 2, :], oT[:, 2 * j:2 * j + 2, :],
                                  r[:].rearrange("p (g s) -> p g s", g=2), ALU.mult).then_inc(taken, 1)
            if job == "wo":
                dve.wait_ge(x_shifted, bt + 1)
                dve.scalar_tensor_tensor(out=xp, in0=r[:].rearrange("p (t d) -> p t d", t=TT), scalar=gates[:, 1:2],
                                         in1=x_all[:, bass.ds(bt * TT, TT), :], op0=ALU.mult,
                                         op1=ALU.add).then_inc(taken, 1)
                f.wait_taken(dve, "wo", bt)
                stats(xp, st2, mv2).then_inc(stats2_ready, 1)
            if job == "rt":
                dve.tensor_tensor(lg[:], r[:, 0:TT * E].rearrange("p (t e) -> p t e", e=E),
                                  gb[:].unsqueeze(1).broadcast_to([P, TT, E]), ALU.add).then_inc(taken, 1)
                f.wait_taken(dve, "rt", bt)
                step.done(dve.tensor_reduce(r1[:, 4, :], lg[:], AX.X, ALU.max))
                dve.tensor_tensor(lg[:], lg[:], r1[:, 4, :].unsqueeze(2).broadcast_to([P, TT, E]),
                                  ALU.subtract).then_inc(shifted_ready, 1)
            if job == "la":
                dve.wait_ge(exp_ready, bt + 1)
                choose()
                for c in range(2):
                    ins = dve.tensor_tensor(am[:, :, c, :].rearrange("p t (e r) -> p t e r", r=R),
                                            r[:, 0:TT * P].rearrange("p (t e r) -> p t e r", t=TT, r=R),
                                            te(oh[:, c, :]).unsqueeze(3).broadcast_to([P, TT, E, R]), ALU.mult)
                ins.then_inc(am_ready, 1)
                dve.wait_ge(am_ready, bt + 1)
                dve.sem_inc(taken, 1)
            if job[0:2] == "up":
                c = int(job[2])
                dve.wait_ge(relu_ready, bt * FC + c + 1)
                dve.scalar_tensor_tensor(out=hT[:, c, :], in0=r[:, 0:S], scalar=nbi[:, c:c + 1], in1=t2[:, c % 2, :],
                                         op0=ALU.max, op1=ALU.add).then_inc(taken, 1)
            if job == "down":
                dve.wait_ge(final_stored, bt * 16 + 16)
                dve.tensor_tensor(ob, r[:].rearrange("p (t d) -> p t d", t=TT),
                                  crow3[:].unsqueeze(1).broadcast_to([P, TT, D]), ALU.add).then_inc(taken, 1)
                f.wait_taken(dve, "down", bt)
                for t in range(TT):
                    ins = dve.scalar_tensor_tensor(out=ob[:, t, :], in0=ob[:, t, :], scalar=r1[:, 5, t:t + 1],
                                                   in1=xp[:, t, :], op0=ALU.mult, op1=ALU.add)
                ins.then_inc(final_ready, 1)

        ins = dve.tensor_copy(biB, bi[:].unsqueeze(2).broadcast_to([P, FC, P]))
        ins.then_inc(biB_done, 1)
        combine(0)
        normalise(0)
        dve.wait_ge(crow3_ready, 1)
        dve.scalar_tensor_tensor(out=crow3[:], in0=crow3[:], scalar=2.0, in1=T_BANK[0][:, 0:D], op0=ALU.mult,
                                 op1=ALU.add).then_inc(weights_done, 1)
        dve.wait_ge(weights_done, 4)
        dve.wait_ge(consts_done, 2)
        consume(fam["proj"], "v0", 0)

        def batch(b, post, front, heads=True):
            for s in range(NH):
                H = b * NH + s
                if s >= 2 and heads or s < 2 and later(b):
                    dve.wait_ge(pT_ready, H - 1)
                    if later(b) or s - 2 >= NPT1:
                        dve.wait_ge(out_ready, b * NP1 + (s - 2) // G1 - 1)
                    dve.tensor_copy(pT[:, (s - 2) % NPT1, :], T_BANK[s % 2][:]).then_inc(pT_taken, 1)
                if heads:
                    dve.wait_ge(scores_ready, H + 1)
                    dve.tensor_reduce(nmax[:, s % 4, :], S_BANK[s % 2][:].rearrange("p (t k) -> p t k", t=TT), AX.X,
                                      ALU.max, negate=True).then_inc(nmax_ready, 1)
                if s == 1 and later(b):
                    dve.wait_ge(probs_ready, b * NH)
                    invert(1)
                if s == 9 and heads:
                    dve.wait_ge(probs_ready, b * NH + 8)
                    invert(0)
                if s == 5 and front:
                    combine(b + 1)
                if s == 7 and post:
                    normalise3(b - 1)
                if s == 8 and front:
                    normalise(b + 1)
                for f, job, bt in due(SCHED_C, s, b, post, heads, front):
                    consume(fam[f], job, bt)

        batch(0, False, True)
        with dve.Fori(1, B - 1) as b:
            step.loop(b - 1, 23)
            batch(b, True, True)
        step.end(B - 2)
        batch(B - 1, True, False)
        batch(B, True, False, heads=False)

    @block.tensor
    def _(pe):
        mm = pe.matmul
        pe.wait_ge(w1_loaded, W1_LOADS)

        def fill(f, job, bt):
            r = f.bank(job)
            f.wait_free(pe, job, bt)
            if job == "xT":
                pe.wait_ge(xn_ready, bt + 1)
            if job == "x3T":
                pe.wait_ge(x3_ready, bt + 1)
            if job in ("xT", "x3T"):
                a = xn if job == "xT" else x3n
                for c in range(DC):
                    for t in range(TT):
                        o = c * S + t * P
                        ins = pe.transpose(r[:, o:o + P], a[:, t, c * P:c * P + P], ident[:])
            if job[0:2] == "qk":
                p = int(job[2])
                pe.wait_ge(ctx_loaded, bt * 16 + 16)
                for j, (wt, a) in enumerate(((wq, xnT), (wkv, cT))):
                    for d in range(DC):
                        ins = mm(r[:, j * S:j * S + S], wt[:, d, p * P:p * P + P], a[:, d, :],
                                 start=d == 0, stop=d == DC - 1)
            if job[0] == "v":
                p = int(job[1])
                for t in range(TT):
                    for d in range(DC):
                        o = NH * HD1 + p * P
                        ins = mm(r[:, t * P:t * P + P], cT[:, d, t * P:t * P + P], wkv[:, d, o:o + P],
                                 start=d == 0, stop=d == DC - 1)
            if job == "rT":
                pe.wait_ge(rinv_ready, bt * 2 + 2)
                for t in range(TT):
                    ins = mm(r[0:NH, t * P:t * P + P], rinv[:, t, :], ident[:], start=True, stop=True)
            if job[0:2] == "bc":
                j = int(job[2])
                f.wait_other(pe, job, "rT", bt)
                for i in range(2):
                    ins = mm(r[:, i * S:i * S + S], sel[:, 2 * j + i, :], rT[:], start=True, stop=True)
            if job == "wo":
                f.wait_other(pe, job, "bc3", bt)
                for t in range(TT):
                    for g in range(NP1):
                        ins = mm(r[:, t * D:t * D + D], oTn[:, g, t * P:t * P + P], wo[:, g, :],
                                 start=g == 0, stop=g == NP1 - 1)
            if job in ("rt", "la"):
                f.wait_other(pe, job, "x3T", bt)
                wt, n = (gw, E) if job == "rt" else (lA, P)
                for t in range(TT):
                    for c in range(DC):
                        ins = mm(r[:, t * n:t * n + n], x3T[:, c, t * P:t * P + P], wt[:, c, :],
                                 start=c == 0, stop=c == DC - 1)
            if job == "laT":
                pe.wait_ge(am_ready, bt + 1)
                for c in range(2):
                    for t in range(TT):
                        o = c * S + t * P
                        ins = pe.transpose(r[:, o:o + P], am[:, t, c, :], ident[:])
            if job[0:2] == "up":
                c = int(job[2])
                o = slice(c * P, c * P + P)
                if c == 0:
                    f.wait_other(pe, job, "laT", bt)
                for d in range(DC):
                    mm(r[:], wi[:, d, o], x3T[:, d, :].unsqueeze(1).broadcast_to([P, 2, S]), start=d == 0, stop=False)
                ins = mm(r[:], lB[:, o], amT.rearrange("p c s -> p (c s)"), start=False, stop=True)
            if job == "down":
                f.wait_other(pe, job, f"up{FC - 1}", bt)
                for t in range(TT):
                    for c in range(FC):
                        ins = mm(r[:, t * D:t * D + D], hT[:, c, t * P:t * P + P], wd[:, c, :],
                                 start=c == 0, stop=c == FC - 1)
            ins.then_inc(f.ready_of(job), 1)

        pe.wait_ge(biB_done, 1)
        for c in range(FC):
            ins = mm(T_BANK[0][:, 0:D], biB[:, c, :], wd[:, c, :], start=c == 0, stop=c == FC - 1)
        ins.then_inc(crow3_ready, 1)
        pe.wait_ge(weights_done, 4)
        pe.wait_ge(consts_done, 2)
        for job in ("xT", "qk0", "v0"):
            fill(fam["proj"], job, 0)

        def turn(b, s):
            H = b * NH + s
            pe.wait_ge(probs_ready, H - 1)
            if later(b) or s >= 4:
                pe.wait_ge(pT_taken, H - 3)
            o, p = T_BANK[s % 2], prob[:, s % 2, :]
            for kt in range(TT):
                for t in range(TT):
                    ins = pe.transpose(o[:, kt * S + t * P:kt * S + t * P + P],
                                       p[:, t * S + kt * P:t * S + kt * P + P], ident[:])
            ins.then_inc(pT_ready, 1)

        def scores(b, s):
            p, j = s // 2, s % 2
            if j == 0:
                fam["proj"].wait_taken(pe, f"qk{p}", b)
            rows = slice(HD1 * j, HD1 * j + HD1)
            q, k = qk[rows, p % 2, 0:S], qk[rows, p % 2, S:2 * S]
            for t in range(TT):
                ins = mm(S_BANK[s % 2][:, t * S:t * S + S], q[:, t * P:t * P + P], k, start=True, stop=True)
            ins.then_inc(scores_ready, 1)

        def values(b, s):
            g = (s - 4) % NH // G1
            G = b * NP1 + (s - 4) // G1
            pe.wait_ge(pT_taken, b * NH + s - 2)
            if later(b) or g >= 1:
                pe.wait_ge(out_taken, G)
            fam["proj"].wait_taken(pe, f"v{g}", b if s >= 4 else b - 1)
            for kt in range(TT):
                for j in range(G1):
                    ins = mm(O_BANK[HD1 * j:HD1 * j + HD1, 0:S], V[:, g % 4, kt, HD1 * j:HD1 * j + HD1],
                             pT[:, (2 * g + j) % NPT1, kt * S:kt * S + S], start=kt == 0, stop=kt == TT - 1)
            ins.then_inc(out_ready, 1)

        def batch(b, post, front, heads=True):
            for s in range(NH):
                if s >= 2 and heads or s < 2 and later(b):
                    turn(b, s)
                if heads:
                    scores(b, s)
                for f, job, bt in due(SCHED_C, s, b, post, heads, front):
                    fill(fam[f], job, bt)
                if s % G1 == 0 and (s >= 4 and heads or s < 4 and later(b)):
                    values(b, s)

        batch(0, False, True)
        with pe.Fori(1, B - 1) as b:
            batch(b, True, True)
        batch(B - 1, True, False)
        batch(B, True, False, heads=False)


def phase_bc(nc, v):
    with ExitStack() as ctx:
        sb = lambda name, shape: ctx.enter_context(nc.sbuf_tensor(name, shape, F32))
        sem = lambda name: ctx.enter_context(nc.semaphore(name))
        w = dict(wq=sb("wq1", [P, DC, NH * HD1]), wkv=sb("wkv1", [P, DC, 2 * NH * HD1]), wo=sb("wo1", [P, NH // G1, D]),
                 wi=sb("wi1", [P, DC, FF]), wd=sb("wd1", [P, FC, D]), lB=sb("lB1", [P, FF]), lA=sb("lA1", [P, DC, E * R]),
                 gw=sb("gw1", [P, DC, E]), gb=sb("gb1", [P, E]), crow1=sb("crow1", [P, D]), crow3=sb("crow3", [P, D]),
                 bi=sb("bi1", [P, FC]))
        w1_loaded = sem("w1_loaded")
        rows = lambda a: a.rearrange("(c p) n -> p c n", p=P)
        w1 = [(w["wq"][:], rows(v["Wq1"])), (w["wkv"][:], rows(v["Wkv1"])), (w["wo"][:], rows(v["Wo1"])),
              (w["wi"][:], rows(v["wiT"])), (w["wd"][:], rows(v["woT"])), (w["lB"][:], v["loraB"]),
              (w["lA"][:], rows(v["loraAT"])), (w["gw"][:], rows(v["gate_wT"])),
              (w["gb"][:], v["gate_b"].partition_broadcast(P)), (w["crow1"][:], v["bo1"].partition_broadcast(P)),
              (w["crow3"][:], v["bo3"].partition_broadcast(P)), (w["bi"][:], v["bi"].rearrange("(c p) -> p c", p=P))]
        with ExitStack() as b_ctx:
            phase_b(nc, v, b_ctx, w1, w1_loaded)
        with ExitStack() as c_ctx:
            phase_c(nc, v, c_ctx, w, w1_loaded)


_INS = ["x", "ctxT", "g_x", "g_f", "Wq0", "bq0", "Wk0", "bk0", "Wv0", "bv0", "Wo0", "bo0", "nscale", "w_routerT",
        "w_upT", "w_downT", "Wq1", "Wkv1", "Wo1", "bo1", "wiT", "bi", "woT", "bo3", "loraAT", "loraB", "gate_wT",
        "gate_b"]


def laid_out(i):
    t = lambda a, *axes: np.ascontiguousarray(np.transpose(np.asarray(a), axes or None))
    n = lambda a: np.ascontiguousarray(np.asarray(a))
    return dict(
        x=n(i["x"]), ctxT=t(i["ctx_1024"], 0, 2, 1), g_x=n(i["g_xattn"]), g_f=n(i["g_ffn"]),
        Wq0=n(i["L0_xattn_Wq"]), bq0=n(i["L0_xattn_bq"]), Wk0=n(i["L0_xattn_Wk"]), bk0=n(i["L0_xattn_bk"]),
        Wv0=n(i["L0_xattn_Wv"]), bv0=n(i["L0_xattn_bv"]), Wo0=n(i["L0_xattn_Wo"]), bo0=n(i["L0_xattn_bo"]),
        nscale=n(i["L0_ffn_norm_scale"]), w_routerT=t(i["L0_ffn_w_router"]),
        w_upT=t(i["L0_ffn_w_up"], 0, 2, 1), w_downT=t(i["L0_ffn_w_down"], 0, 2, 1),
        Wq1=n(i["L1_xattn_Wq"]), Wkv1=n(i["L1_xattn_Wkv"]), Wo1=n(i["L1_xattn_Wo"]), bo1=n(i["L1_xattn_bo"]),
        wiT=t(i["L1_ffn_wi"]), bi=n(i["L1_ffn_bi"]), woT=t(i["L1_ffn_wo"]), bo3=n(i["L1_ffn_bo"]),
        loraAT=t(np.reshape(np.asarray(i["L1_ffn_lora_A"]), (E * R, D))),
        loraB=np.reshape(t(i["L1_ffn_lora_B"], 0, 2, 1), (E * R, FF)),
        gate_wT=t(i["L1_ffn_gate_w"]), gate_b=n(i["L1_ffn_gate_b"]))


def kernel(**inputs):
    import concourse.bacc as bacc
    from concourse.bass_utils import run_bass_kernel_spmd

    nc = bacc.Bacc("TRN2", target_bir_lowering=False, num_devices=1)
    arrays = laid_out(inputs)
    args = [nc.dram_tensor(k, arrays[k].shape, mybir.dt.from_np(arrays[k].dtype), kind="ExternalInput").ap()
            for k in _INS]
    out = nc.dram_tensor("out", [B, S, D], F32, kind="ExternalOutput").ap()
    build(nc, *args, out)
    return run_bass_kernel_spmd(nc, [arrays], core_ids=[0]).results[0]["out"]
```

```python
from contextlib import ExitStack

import numpy as np

import concourse.bass as bass
from concourse import mybir
from concourse.alu_op_type import AluOpType as ALU

ACT = mybir.ActivationFunctionType
F32 = mybir.dt.float32
F32R = mybir.dt.float32r
BF16 = mybir.dt.bfloat16
I32 = mybir.dt.int32
U32 = mybir.dt.uint32
AX = mybir.AxisListType

P = 128
B, S, D = 8, 256, 256
TT = S // P
DC = D // P
NT = B * TT
NH = 16
HD0, HD1 = 16, 64
SLOT0 = 32
G0, G1 = 4, 2
CHUNK = 64
E = 8
HID = 512
FF = 1024
FC = FF // P
HC = HID // P
R = 16
LG = E * R + E
CAP = S * B + P
PAD_ROW = E * CAP
TILES = (2 * S * B + E * (P - 1)) // P
ROWS_IN, ROWS_OUT = PAD_ROW + P, TILES * P
NPT = 8
LN_EPS, RMS_EPS = 1e-5, 1e-6
NEG = -1e9
LOWER = -1e30

PROJ_A = ["xT", "qk0", "v0", "qk1", "v1"]
POST_A = ["rT", "bc0", "bc1", "wo0", "wo1", "x2T", "rt", "rank"]
SCHED_A = [(1, "proj", "qk1", 0), (5, "proj", "v1", 0), (7, "proj", "xT", 1), (10, "proj", "qk0", 1),
           (13, "proj", "v0", 1), (3, "post", "rT", -1), (4, "post", "bc0", -1), (5, "post", "bc1", -1),
           (6, "post", "wo0", -1), (7, "post", "wo1", -1), (10, "post", "x2T", -1), (12, "post", "rt", -1),
           (14, "post", "rank", -1)]
PROJ_C = ["xT", "qk0", "vv0", "qk1", "qk2", "vv1", "qk3", "qk4", "vv2", "qk5", "qk6", "vv3", "qk7"]
POST_C = ["rT"] + [f"bc{j}" for j in range(4)] + ["wo0", "wo1", "x3T", "rl", "laT"]
FFN_C = [j for g in range(FC // 2) for j in (f"base{g}", f"lora{2 * g}", f"lora{2 * g + 1}")] + ["down0", "down1"]
POST_C_SLOTS = [2, 3, 4, 5, 6, 7, 8, 10, 11, 14]
FFN_C_SLOTS = [13, 15, 1, 1, 2, 2, 3, 4, 5, 5, 6, 6, 9, 12]
SCHED_C = ([(2 * p - 2, "proj", f"qk{p}", 0) for p in range(1, 8)]
           + [(4 * k - 1, "proj", f"vv{k}", 0) for k in range(1, 4)]
           + [(13, "proj", "xT", 1), (14, "proj", "qk0", 1), (15, "proj", "vv0", 1)]
           + [(s, "post", j, -1) for s, j in zip(POST_C_SLOTS, POST_C)]
           + [(s, "ffn", j, -1 if i < 2 else -2) for i, (s, j) in enumerate(zip(FFN_C_SLOTS, FFN_C))])
DVE_C = {"combine_first": 1, "combine_second": 5, "stats": 5, "normalise": 6, "normalise3": 9, "choose_first": 12}
DVE_A = {"stats": 2, "normalise": 4, "expert_rows": 9, "second_choice": 12}
SCATTER_SLOTS = {14: (0, 1), 15: (2, 3)}


class Family:

    def __init__(self, names, banks, ready, taken):
        self.names, self.banks, self.ready, self.taken = names, banks, ready, taken

    def place(self, job, batch):
        j, n = self.names.index(job), len(self.banks)
        k = j % n
        return k, batch * ((len(self.names) - k + n - 1) // n) + j // n

    def bank(self, job):
        return self.banks[self.names.index(job) % len(self.banks)]

    def wait_free(self, eng, job, batch):
        k, n = self.place(job, batch)
        eng.wait_ge(self.taken[k], n + 1)

    def wait_ready(self, eng, job, batch):
        k, n = self.place(job, batch)
        eng.wait_ge(self.ready[k], n + 1)

    def wait_taken(self, eng, job, batch):
        k, n = self.place(job, batch)
        eng.wait_ge(self.taken[k], n + 2)

    def wait_other(self, eng, job, other, batch):
        if self.bank(job) is not self.bank(other):
            self.wait_taken(eng, other, batch)

    def ready_of(self, job):
        return self.ready[self.names.index(job) % len(self.banks)]

    def taken_of(self, job):
        return self.taken[self.names.index(job) % len(self.banks)]


def due(sched, slot, b, post, own, front, tail=False):
    return [(f, j, b + d) for s, f, j, d in sched if s == slot and (tail, post, own, front)[d + 2]]


class Steps:

    def __init__(self, eng, sem):
        self.eng, self.sem, self.n, self.turn = eng, sem, 0, 0

    def loop(self, i, per):
        self.turn, self.per, self.n0 = i * per, per, self.n

    def end(self, times):
        assert self.n - self.n0 == self.per, (self.n - self.n0, self.per)
        self.n, self.turn = self.n0 + times * self.per, 0

    def done(self, ins):
        ins.then_inc(self.sem, 1)
        self.n += 1
        self.eng.wait_ge(self.sem, self.n + self.turn)

    def hold(self):
        self.eng.sem_inc(self.sem, 1)
        self.n += 1


def build(nc, x, ctxT, g_x, g_f, Wq0, bq0, Wk0, bk0, Wv0, bv0, Wo0, bo0, nscale, w_routerT, w_upT, w_downT,
          Wq1, Wkv1, Wo1, bo1, wiT, bi, woT, bo3, loraAT, loraB, gate_wT, gate_b, out):
    with ExitStack() as whole:
        whole.enter_context(nc.allow_non_contiguous_dma(reason="small vectors onto partitions"))
        sem = lambda name: whole.enter_context(nc.semaphore(name))
        keep = lambda name, shape, dt=F32: whole.enter_context(nc.sbuf_tensor(name, shape, dt))
        bank = [whole.enter_context(nc.psum_tensor(f"bank{i}", [P, 512], F32)) for i in range(8)]
        rows_in = nc.dram_tensor("rows_in", [ROWS_IN, D], F32, kind="Internal").ap()
        rows_out = nc.dram_tensor("rows_out", [ROWS_OUT, D], F32, kind="Internal").ap()

        x_all = keep("x_all", [P, NT, D])
        ident = keep("ident", [P, P])
        gates = keep("gates", [P, 4])
        ns = keep("ns", [P, DC])
        gap = keep("gap", [P, NT])
        mix = keep("mix", [P, 2, NT])
        pos_all = keep("pos_all", [P, 2, NT], U32)
        base = keep("base", [P, E])
        row_tab = keep("row_tab", [1, 40], I32)
        exp_tab = keep("exp_tab", [1, 40], I32)
        nhalf = keep("nhalf", [P, TT])

        w = dict(wq=keep("wq1", [P, DC, NH * HD1]), wk=keep("wk1", [P, DC, NH * HD1]), gb=keep("gb1", [P, E]),
                 crow1=keep("crow1", [P, D]), crow3=keep("crow3", [P, D]), bi=keep("bi1", [P, FC]))

        moe_loaded = sem("moe_loaded")
        pads_done = sem("pads_done")
        scattered = sem("scattered")
        tables_done = sem("tables_done")
        mixes_done = sem("mixes_done")

        w1_loaded = sem("w1_loaded")
        with ExitStack() as experts:
            w_up = experts.enter_context(nc.sbuf_tensor("w_up", [P, E * DC * 2 * HID], F32))
            w_dn = experts.enter_context(nc.sbuf_tensor("w_dn", [P, E * HC * D], F32))
            tab, tab2 = (experts.enter_context(nc.sbuf_tensor(n, [P, 40 * E], F32)) for n in ("tab", "tab2"))
            small = experts.enter_context(nc.sbuf_tensor("small", [P, 160], F32))
            w_up_v = w_up[:].rearrange("p (e c h) -> p e c h", e=E, c=DC)
            w_dn_v = w_dn[:].rearrange("p (e c h) -> p e c h", e=E, c=HC)
            phase_a(nc, locals())
            phase_b(nc, locals())
        phase_c(nc, locals())


def phase_a(nc, v):
    x, ctxT, x_all, bank, ident, gates, ns = (v[k] for k in ("x", "ctxT", "x_all", "bank", "ident", "gates", "ns"))
    gap, mix, pos_all, base, row_tab, exp_tab, nhalf, tab, tab2, small = (v[k] for k in (
        "gap", "mix", "pos_all", "base", "row_tab", "exp_tab", "nhalf", "tab", "tab2", "small"))
    rows_in = v["rows_in"]
    moe_loaded, pads_done, scattered, tables_done, mixes_done = (v[k] for k in (
        "moe_loaded", "pads_done", "scattered", "tables_done", "mixes_done"))
    with ExitStack() as ctx:
        sb = lambda name, shape, dt=F32: ctx.enter_context(nc.sbuf_tensor(name, shape, dt))
        sem = lambda name: ctx.enter_context(nc.semaphore(name))

        wq, wk, wv = (sb(n, [P, DC, D]) for n in ("wq0", "wk0", "wv0"))
        wo = sb("wo0", [P, G0, D])
        bvs = sb("bvs", [P, G0])
        bqk = sb("bqk0", [P, 2, DC])
        wr = sb("wr", [P, DC, E])
        crow = sb("crow0", [P, D])
        head_mask = sb("head_mask", [P, E])
        sel = sb("sel0", [3 * NH, G0, P], F32R)
        tri = sb("tri", [P, P], BF16)
        ones = sb("ones", [P, P], BF16)
        rev = sb("rev", [P, TT, E])
        xn = sb("xn0", [P, TT, D])
        xnT = sb("xnT0", [P, DC, S])
        cT = sb("cT0", [P, DC, S])
        qT = sb("qT0", [P, DC, S])
        kT = sb("kT0", [P, DC, S])
        qz = sb("qz", [P, 8, S])
        V = sb("V0", [P, TT, NH, SLOT0])
        prob = sb("prob0", [P, 4, 384])
        pT = sb("pT0", [P, NPT, 384])
        nmax = sb("nmax0", [P, 4, TT])
        den = sb("den0", [P, TT, NH])
        rinv = sb("rinv0", [P, TT, NH])
        rT = sb("rT0", [3 * NH, S], F32R)
        oT = sb("oT0", [P, G0, S])
        oTn = sb("oTn0", [P, G0, S])
        st = sb("st0", [P, TT, 6])
        mv = sb("mv0", [P, TT, 2])
        st2 = sb("st02", [P, TT, 6])
        mv2 = sb("mv02", [P, TT, 2])
        lnw = sb("lnw0", [P, 2, TT])
        lnw2 = sb("lnw02", [P, 6, TT])
        xp = sb("xp", [P, TT, D])
        xs = sb("xs", [P, TT, D])
        xt = sb("xt0", [P, TT, D])
        one_sel = xs[0:NH].rearrange("p t (j d) -> p (t j d)", d=SLOT0).rearrange("p (g n) -> p g n", g=G0)
        zeros = xp[0:3 * NH].rearrange("p t d -> p (t d)")
        bvb = xt[:].rearrange("p t d -> p (t d)").rearrange("p (g n) -> p g n", g=G0)
        x2T = sb("x2T", [P, DC, S])
        lg = sb("lg0", [P, TT, E])
        rw = sb("rw0", [P, 5, TT * E])
        r1 = sb("r10", [P, 4, TT])
        oh = sb("oh0", [P, 2, TT * E])
        hot = sb("hot", [P, TT * E], BF16)
        pos4 = sb("pos4", [P, 2 * TT], U32)
        posf = sb("posf", [P, 2, TT])
        credit = sb("credit", [P, 4])
        zrow = sb("zrow", [P, D])
        padi = sb("padi", [1, E], I32)

        w_loaded = sem("w_loaded")
        wo_loaded = sem("wo_loaded")
        x0_loaded, x_loaded, ctx_loaded = sem("x0_loaded"), sem("x_loaded"), sem("ctx_loaded")
        small_loaded = sem("small_loaded")
        consts_done = sem("consts_done")
        zeroed = sem("zeroed")
        gates_done = sem("gates_done")
        crow_done = sem("crow_done")
        bvb_done = sem("bvb_done")
        scores_ready, nmax_ready, probs_ready = sem("scores_ready"), sem("nmax_ready"), sem("probs_ready")
        pT_ready, pT_taken = sem("pT_ready"), sem("pT_taken")
        out_ready, out_taken = sem("out_ready"), sem("out_taken")
        qz_ready, rinv_ready = sem("qz_ready"), sem("rinv_ready")
        stats_ready, xn_ready, x_shifted = sem("stats_ready"), sem("xn_ready"), sem("x_shifted")
        root_ready, root2_ready = sem("root_ready"), sem("root2_ready")
        xt_ready, xp_used = sem("xt_ready"), sem("xp_used")
        stats2_ready, xs_ready = sem("stats2_ready"), sem("xs_ready")
        hot_ready, pos_ready, padded = sem("hot_ready"), sem("pos_ready"), sem("padded")
        vec_step, pool_step, act_step = sem("vec_step_a"), sem("pool_step_a"), sem("act_step_a")

        S_BANK, T_BANK, O_BANK = bank[0:4], bank[4], bank[5]
        fam = {"proj": Family(PROJ_A, [bank[6]], [sem("proj_ready")], [sem("proj_taken")]),
               "post": Family(POST_A, [bank[7]], [sem("post_ready")], [sem("post_taken")])}
        crow_ready, sel_done = sem("crow_ready"), sem("sel_done0")
        CONSTS = 7
        block = ctx.enter_context(nc.Block())

        @block.sync
        def _(sp):
            xv = x.rearrange("b (t p) d -> p (b t) d", p=P)
            cv = ctxT.rearrange("b (c p) s -> b p c s", p=P)
            sp.dma_start(x_all[:, 0:TT, :], xv[:, 0:TT, :]).then_inc(x0_loaded, 16)
            sp.dma_start(cT[:], cv[0]).then_inc(ctx_loaded, 16)
            for t, w in ((wq, v["Wq0"]), (wk, v["Wk0"]), (wv, v["Wv0"])):
                sp.dma_start(t[:], w.rearrange("(c p) n -> p c n", p=P)).then_inc(w_loaded, 16)
            for j, w in enumerate((v["bq0"], v["bk0"])):
                sp.dma_start(bqk[:, j, :], w.rearrange("(c p) -> p c", p=P)).then_inc(w_loaded, 16)
            sp.dma_start(x_all[:, TT:NT, :], xv[:, TT:NT, :]).then_inc(x_loaded, 16)
            sp.dma_start(wr[:], v["w_routerT"].rearrange("(c p) n -> p c n", p=P)).then_inc(w_loaded, 16)
            sp.wait_ge(wo_loaded, 16 * 2 * G0)
            sp.wait_ge(x_loaded, 16)
            for e in range(E):
                sp.dma_start(v["w_up_v"][:, e], v["w_upT"][e].rearrange("(c p) h -> p c h", p=P)).then_inc(moe_loaded, 16)
                sp.dma_start(v["w_dn_v"][:, e], v["w_downT"][e].rearrange("(c p) d -> p c d", p=P)).then_inc(moe_loaded, 16)

            def next_context(b):
                fam["proj"].wait_ready(sp, "v1", b)
                sp.dma_start(cT[:], cv[bass.ds(b + 1, 1)].rearrange("o p c s -> (o p) c s")).then_inc(ctx_loaded, 16)

            next_context(0)
            with sp.Fori(1, B - 1) as b:
                next_context(b)
            sp.wait_ge(tables_done, 2)
            sp.wait_ge(pads_done, 1)
            for e in range(E):
                row = sp.value_load(padi[0:1, e:e + 1], min_val=0, max_val=PAD_ROW - P)
                sp.dma_start(rows_in[bass.ds(row, P), :], zrow[:]).then_inc(padded, 16)
            sp.wait_ge(padded, 16 * E)

        @block.gpsimd
        def _(pool):
            step = Steps(pool, pool_step)
            pool.memset(nhalf[:], -0.5).then_inc(consts_done, 1)
            step.done(pool.memset(ident[:], 1.0))
            pool.affine_select(out=ident[:], in_=ident[:], compare_op=ALU.is_equal, fill=0.0, base=0,
                               pattern=[[-1, P]], channel_multiplier=1).then_inc(consts_done, 1)
            step.done(pool.memset(head_mask[:], HD0 ** -0.5))
            step.done(pool.affine_select(out=head_mask[:], in_=head_mask[:], compare_op=ALU.is_ge, fill=0.0, base=0,
                                         pattern=[[-HD0, E]], channel_multiplier=1))
            pool.affine_select(out=head_mask[:], in_=head_mask[:], compare_op=ALU.is_ge, fill=0.0, base=HD0 - 1,
                               pattern=[[HD0, E]], channel_multiplier=-1).then_inc(consts_done, 1)
            step.done(pool.memset(one_sel, 1.0))
            sv = one_sel.rearrange("h g (j d) -> h g j d", j=G0)
            pool.affine_select(out=sv, in_=sv, compare_op=ALU.is_equal, fill=0.0, base=0,
                               pattern=[[-G0, G0], [-1, G0], [0, SLOT0]], channel_multiplier=1).then_inc(consts_done, 1)
            pool.memset(ones[:], 1.0).then_inc(consts_done, 1)
            step.done(pool.memset(tri[:], 1.0))
            pool.affine_select(out=tri[:], in_=tri[:], compare_op=ALU.is_gt, fill=0.0, base=0,
                               pattern=[[1, P]], channel_multiplier=-1).then_inc(consts_done, 1)
            pool.iota(rev[:], pattern=[[0, TT], [-1, E]], base=E, channel_multiplier=0,
                      allow_small_or_imprecise_dtypes=True).then_inc(consts_done, 1)
            pool.iota(base[:], pattern=[[CAP, E]], base=0, channel_multiplier=0,
                      allow_small_or_imprecise_dtypes=True)
            pool.iota(tab[:, 0:E * 16].rearrange("p (e j) -> p e j", j=16), pattern=[[0, E], [P, 16]], base=0,
                      channel_multiplier=0, allow_small_or_imprecise_dtypes=True)
            pool.iota(tab2[:].rearrange("p (i e) -> p i e", e=E), pattern=[[1, 40], [0, E]], base=0,
                      channel_multiplier=0, allow_small_or_imprecise_dtypes=True)
            pool.iota(small[:, 0:40], pattern=[[P, 40]], base=0, channel_multiplier=0,
                      allow_small_or_imprecise_dtypes=True).then_inc(tables_done, 1)

            def root(w, m, eps):
                step.hold()
                step.done(pool.tensor_scalar(w[:, 0, :], m[:, :, 1], eps, None, ALU.add))
                return pool.tensor_tensor(w[:, 1, :], w[:, 0, :], nhalf[:], ALU.pow)

            def front_root(b1):
                pool.wait_ge(stats_ready, b1 + 1)
                root(lnw, mv, LN_EPS).then_inc(root_ready, 1)

            def front_shift(b1):
                xb = x_all[:, bass.ds(b1 * TT, TT), :]
                pool.wait_ge(xn_ready, b1 + 1)
                step.hold()
                pool.tensor_tensor(xb, xb, crow[:].unsqueeze(1).broadcast_to([P, TT, D]), ALU.add).then_inc(x_shifted, 1)

            def post_root(b0):
                w = lnw2
                pool.wait_ge(stats2_ready, b0 + 1)
                step.done(root(w, mv2, LN_EPS))
                step.done(pool.tensor_tensor(w[:, 2, :], w[:, 1, :], w[:, 1, :], ALU.mult))
                step.done(pool.tensor_tensor(w[:, 2, :], w[:, 2, :], mv2[:, :, 1], ALU.mult))
                step.hold()
                step.done(pool.tensor_scalar(w[:, 2, :], w[:, 2, :], RMS_EPS, None, ALU.add))
                step.done(pool.tensor_tensor(w[:, 3, :], w[:, 2, :], nhalf[:], ALU.pow))
                pool.tensor_tensor(w[:, 4, :], w[:, 3, :], w[:, 1, :], ALU.mult).then_inc(root2_ready, 1)
                pool.tensor_scalar(w[:, 5, :], w[:, 1, :], gates[:, 2:3], None, ALU.mult).then_inc(root2_ready, 1)

            def post_skip(b0):
                pool.wait_ge(xt_ready, b0 + 1)
                step.hold()
                pool.tensor_tensor(x_all[:, bass.ds(b0 * TT, TT), :], xp[:], xt[:], ALU.add).then_inc(xp_used, 1)

            def scatter(b0, parts):
                pool.wait_ge(pos_ready, b0 + 1)
                step.hold()
                for j in parts:
                    pool.indirect_dma_start(rows_in, bass.IndirectOffsetOnAxis(ap=pos4[:, j:j + 1], axis=0),
                                            xs[:, j % TT, :], None).then_inc(scattered, 16)

            def batch(b, post, front):
                for s in range(NH):
                    if s == 1 and front:
                        front_root(b + 1)
                    if s == 5 and front:
                        front_shift(b + 1)
                    if s == 6 and post:
                        post_root(b - 1)
                    if s == 9 and post:
                        post_skip(b - 1)
                    if post and s in SCATTER_SLOTS:
                        scatter(b - 1, SCATTER_SLOTS[s])

            pool.memset(zrow[:], 0.0).then_inc(pads_done, 1)
            pool.wait_ge(pads_done, 1)
            pool.dma_start(rows_in[PAD_ROW:ROWS_IN, :], zrow[:]).then_inc(scattered, 16)
            pool.wait_ge(consts_done, CONSTS)
            front_root(0)
            pool.wait_ge(crow_done, 1)
            front_shift(0)
            batch(0, False, True)
            with pool.Fori(1, B - 1) as b:
                step.loop(b - 1, 14)
                batch(b, True, True)
            step.end(B - 2)
            batch(B - 1, True, False)
            batch(B, True, False)
            pool.wait_ge(scattered, 16 * (2 * NT + 1))

        @block.scalar
        def _(act):
            act.dma_start(gates[:, 0:2], v["g_x"].partition_broadcast(P)).then_inc(small_loaded, 16)
            act.dma_start(gates[:, 2:4], v["g_f"].partition_broadcast(P)).then_inc(small_loaded, 16)
            act.dma_start(crow[:], v["bo0"].partition_broadcast(P)).then_inc(small_loaded, 16)
            act.dma_start(ns[:], v["nscale"].rearrange("(c p) -> p c", p=P)).then_inc(small_loaded, 16)
            act.wait_ge(zeroed, 2)
            bvv = v["bv0"].rearrange("(h d) -> d h", d=HD0)
            for j in range(G0):
                act.dma_start(wo[SLOT0 * j:SLOT0 * j + HD0, :, :],
                              v["Wo0"].rearrange("(g j d) n -> j d g n", j=G0, d=HD0)[j]).then_inc(wo_loaded, 16)
                act.dma_start(bvs[SLOT0 * j:SLOT0 * j + HD0, :], bvv[:, j:NH:G0]).then_inc(wo_loaded, 16)
            act.wait_ge(small_loaded, 64)
            act.activation(gates[:], gates[:], ACT.Tanh).then_inc(gates_done, 1)

            def consume(f, job, bt):
                r = f.bank(job)
                if job in ("xT", "x2T", "qk0", "qk1", "v0", "v1"):
                    f.wait_ready(act, job, bt)
                if job == "xT":
                    act.copy(xnT[:].rearrange("p c s -> p (c s)"), r[:]).then_inc(f.taken_of(job), 1)
                if job == "x2T":
                    act.mul(x2T[:, 0, :], r[:, 0:S], ns[:, 0:1])
                    act.mul(x2T[:, 1, :], r[:, S:2 * S], ns[:, 1:2]).then_inc(f.taken_of(job), 1)
                if job in ("qk0", "qk1"):
                    c = int(job[2])
                    if later(bt):
                        act.wait_ge(qz_ready, bt * NH - 8 + 8 * c)
                        act.wait_ge(scores_ready, bt * NH - 8 + 8 * c)
                    act.activation(qT[:, c, :], r[:, 0:S], ACT.Identity, bias=bqk[:, 0, c:c + 1])
                    act.activation(kT[:, c, :], r[:, S:2 * S], ACT.Identity,
                                   bias=bqk[:, 1, c:c + 1]).then_inc(f.taken_of(job), 1)
                if job in ("v0", "v1"):
                    c = int(job[1])
                    if later(bt):
                        act.wait_ge(out_ready, bt * G0 - 2 + 2 * c)
                    else:
                        act.wait_ge(zeroed, 3)
                    act.copy(V[:, :, 8 * c:8 * c + 8, 0:HD0],
                             r[:, 0:TT * P].rearrange("p (t h d) -> p t h d", t=TT, h=8)).then_inc(f.taken_of(job), 1)

            def masked_q(h, b):
                if h % 8 == 0:
                    fam["proj"].wait_taken(act, f"qk{h // 8}", b)
                act.mul(qz[:, h % 8, :], qT[:, h // 8, :], head_mask[:, h % 8:h % 8 + 1]).then_inc(qz_ready, 1)

            act.wait_ge(w_loaded, 96)
            for job in ("xT", "qk0"):
                consume(fam["proj"], job, 0)
            act.wait_ge(consts_done, CONSTS)
            for h in range(4):
                masked_q(h, 0)
            consume(fam["proj"], "v0", 0)

            def batch(b, post, front, heads=True):
                for s in range(NH):
                    H = b * NH + s
                    if heads:
                        if later(b) and s == 0:
                            act.wait_ge(rinv_ready, b * 2 - 1)
                        if later(b) and s == 8:
                            act.wait_ge(rinv_ready, b * 2)
                        act.wait_ge(nmax_ready, H + 1)
                        for t, (c0, c1) in enumerate(((0, P), (P, 3 * P))):
                            ins = act.activation(prob[:, s % 4, c0:c1], S_BANK[s % 4][:, c0:c1], ACT.Exp,
                                                 bias=nmax[:, s % 4, t:t + 1], accum_out=den[:, t, s:s + 1])
                        ins.then_inc(probs_ready, 1)
                    if heads and s < NH - 4:
                        masked_q(s + 4, b)
                    if front and s >= NH - 4:
                        masked_q(s + 4 - NH, b + 1)
                    for f, job, bt in due(SCHED_A, s, b, post, heads, front):
                        consume(fam[f], job, bt)
                    if s % G0 == G0 - 1 and (s >= 4 and heads or s < 4 and later(b)):
                        g = (s - 4) % NH // G0
                        act.wait_ge(out_ready, b * G0 + (s - 4) // G0 + 1)
                        if later(b) and s >= 4:
                            fam["post"].wait_taken(act, "bc1", b - 1)
                        act.copy(oT[:, g, :], O_BANK[:, 0:S]).then_inc(out_taken, 1)

            batch(0, False, True)
            with act.Fori(1, B - 1) as b:
                batch(b, True, True)
            batch(B - 1, True, False)
            batch(B, True, False, heads=False)
            act.wait_ge(mixes_done, 1)
            act.activation(gap[:], gap[:], ACT.Exp).then_inc(mixes_done, 1)

        @block.vector
        def _(dve):
            step = Steps(dve, vec_step)
            dve.memset(wo[:], 0.0).then_inc(zeroed, 1)
            dve.memset(bvs[:], 0.0).then_inc(zeroed, 1)
            dve.memset(V[:], 0.0).then_inc(zeroed, 1)
            for o in S_BANK:
                for o1 in (P, 3 * P):
                    dve.memset(o[0:CHUNK, o1 - CHUNK:o1], NEG)
            dve.memset(credit[:, 0:1], 0.0).then_inc(fam["proj"].taken[0], 1)
            dve.memset(credit[:, 2:3], 0.0).then_inc(xp_used, 1)

            def stats(xb, st_, mv_):
                for t in range(TT):
                    ins = dve.bn_stats(st_[:, t, :], xb(t))
                step.done(ins)
                step.hold()
                for t in range(TT):
                    ins = dve.bn_aggr(mv_[:, t, :], st_[:, t, :])
                return ins

            def tile_of(b1):
                return lambda t: x_all[:, bass.ds(b1 * TT + t, 1), :].rearrange("p o d -> p (o d)")

            def normalise(b1):
                dve.wait_ge(root_ready, b1 + 1)
                if later(b1):
                    fam["proj"].wait_ready(dve, "xT", b1 - 1)
                for t in range(TT):
                    ins = dve.tensor_scalar(xn[:, t, :], tile_of(b1)(t), mv[:, t, 0:1], lnw[:, 1, t:t + 1],
                                            ALU.subtract, ALU.mult)
                ins.then_inc(xn_ready, 1)

            def expert_rows(b0):
                dve.wait_ge(root2_ready, 2 * b0 + 2)
                dve.wait_ge(scattered, b0 * (32 * TT) + 16)
                for t in range(TT):
                    ins = dve.tensor_scalar(xs[:, t, :], xp[:, t, :], mv2[:, t, 0:1], lnw2[:, 4, t:t + 1],
                                            ALU.subtract, ALU.mult)
                ins.then_inc(xs_ready, 1)
                dve.wait_ge(xp_used, b0 + 1)
                for t in range(TT):
                    ins = dve.tensor_scalar(xt[:, t, :], xp[:, t, :], mv2[:, t, 0:1], lnw2[:, 5, t:t + 1],
                                            ALU.subtract, ALU.mult)
                ins.then_inc(xt_ready, 1)

            def invert(half):
                h = slice(8 * half, 8 * half + 8)
                dve.reciprocal(rinv[:, :, h], den[:, :, h]).then_inc(rinv_ready, 1)

            def first_of(src, m, one):
                w = rw[:, 0, :].rearrange("p (t e) -> p t e", e=E)
                step.done(dve.tensor_reduce(m, src, AX.X, ALU.max))
                step.done(dve.tensor_tensor(w, src, m.unsqueeze(2).broadcast_to([P, TT, E]), ALU.is_equal))
                step.done(dve.tensor_tensor(w, w, rev[:], ALU.mult))
                step.done(dve.tensor_reduce(r1[:, 3, :], w, AX.X, ALU.max))
                step.done(dve.tensor_tensor(one, rev[:], r1[:, 3, :].unsqueeze(2).broadcast_to([P, TT, E]), ALU.is_equal))

            def te(a):
                return a.rearrange("p (t e) -> p t e", e=E)

            def consume(f, job, bt):
                r = f.bank(job)
                if job in ("rT", "bc0", "bc1", "wo0", "wo1", "rt"):
                    f.wait_ready(dve, job, bt)
                if job == "rT":
                    step.done(dve.tensor_copy(rT[0:NH], r[0:NH, 0:S]))
                    dve.tensor_tensor(rT[2 * NH:3 * NH], r[0:NH, 0:S], rT[0:NH].bitcast(F32),
                                      ALU.subtract).then_inc(f.taken_of(job), 1)
                if job in ("bc0", "bc1"):
                    j = int(job[2])
                    dve.wait_ge(out_taken, bt * G0 + G0)
                    dve.tensor_tensor(oTn[:, 2 * j:2 * j + 2, :], oT[:, 2 * j:2 * j + 2, :],
                                      r[:].rearrange("p (g s) -> p g s", g=2), ALU.mult).then_inc(f.taken_of(job), 1)
                if job in ("wo0", "wo1"):
                    t = int(job[2])
                    if t == 0:
                        dve.wait_ge(x_shifted, bt + 1)
                        dve.wait_ge(xp_used, bt + 1)
                    dve.scalar_tensor_tensor(out=xp[:, t, :], in0=r[:, 0:D], scalar=gates[:, 0:1], in1=tile_of(bt)(t),
                                             op0=ALU.mult, op1=ALU.add).then_inc(f.taken_of(job), 1)
                    f.wait_taken(dve, job, bt)
                    step.done(dve.bn_stats(st2[:, t, :], xp[:, t, :]))
                    step.hold()
                    ins = dve.bn_aggr(mv2[:, t, :], st2[:, t, :])
                    if t == TT - 1:
                        ins.then_inc(stats2_ready, 1)
                if job == "rt":
                    dve.tensor_copy(lg[:].rearrange("p t e -> p (t e)"), r[:, 0:TT * E]).then_inc(f.taken_of(job), 1)
                    f.wait_taken(dve, "rt", bt)
                    first_of(lg[:], r1[:, 0, :], te(oh[:, 0, :]))

            def second_choice(bt):
                l2 = te(rw[:, 1, :])
                step.done(dve.scalar_tensor_tensor(out=l2, in0=te(oh[:, 0, :]), scalar=LOWER, in1=lg[:],
                                                   op0=ALU.mult, op1=ALU.add))
                first_of(l2, r1[:, 1, :], te(oh[:, 1, :]))
                dve.tensor_tensor(hot[:], oh[:, 0, :], oh[:, 1, :], ALU.add).then_inc(hot_ready, 1)
                dve.tensor_tensor(gap[:, bass.ds(bt * TT, TT)], r1[:, 1, :], r1[:, 0, :], ALU.subtract)

            def positions(f, job, bt):
                r = f.bank(job)
                f.wait_ready(dve, job, bt)
                rk = rw[:, 2, :]
                step.done(dve.tensor_tensor(te(rk), te(r[:, 0:TT * E]), base[:].unsqueeze(1).broadcast_to([P, TT, E]),
                                            ALU.add))
                dve.tensor_tensor(base[:], base[:], r[:, TT * E:TT * E + E], ALU.add).then_inc(f.taken_of(job), 1)
                for c in range(2):
                    ins = dve.tensor_tensor(rw[:, 3 + c, :], oh[:, c, :], rk, ALU.mult)
                step.done(ins)
                for c in range(2):
                    ins = dve.tensor_reduce(posf[:, c, :], te(rw[:, 3 + c, :]), AX.X, ALU.add)
                step.done(ins)
                dve.wait_ge(scattered, bt * (32 * TT) + 16)
                dve.tensor_copy(pos_all[:, :, bass.ds(bt * TT, TT)], posf[:])
                dve.tensor_copy(pos4[:], posf[:].rearrange("p c t -> p (c t)")).then_inc(pos_ready, 1)

            dve.wait_ge(wo_loaded, 16 * 2 * G0)
            dve.wait_ge(zeroed, 2)
            for g in range(G0):
                ins = dve.tensor_copy(bvb[:, g, :], bvs[:, g:g + 1].broadcast_to([P, P]))
            ins.then_inc(bvb_done, 1)
            dve.wait_ge(x0_loaded, 16)
            stats(tile_of(0), st, mv).then_inc(stats_ready, 1)
            normalise(0)
            dve.wait_ge(crow_ready, 1)
            dve.wait_ge(gates_done, 1)
            step.done(dve.tensor_tensor(crow[:], crow[:], fam["post"].bank("rT")[:, 0:D], ALU.add))
            dve.tensor_scalar(crow[:], crow[:], gates[:, 0:1], None, ALU.mult).then_inc(crow_done, 1)
            dve.memset(credit[:, 1:2], 0.0).then_inc(fam["post"].taken[0], 1)
            dve.wait_ge(consts_done, CONSTS)
            dve.wait_ge(tables_done, 1)
            step.done(dve.memset(zeros, 0.0))
            dve.tensor_copy(rT[:], zeros[:, 0:S])
            step.done(dve.tensor_copy(sel[:], zeros.rearrange("p (g n) -> p g n", g=G0)))
            dve.tensor_copy(sel[0:NH], one_sel)
            dve.tensor_copy(sel[2 * NH:3 * NH], one_sel).then_inc(sel_done, 1)
            dve.wait_ge(sel_done, 1)

            def batch(b, post, front, heads=True):
                for s in range(NH):
                    H = b * NH + s
                    if heads:
                        dve.wait_ge(scores_ready, H + 1)
                        sc = S_BANK[s % 4]
                        dve.tensor_reduce(nmax[:, s % 4, 0:1], sc[:, 0:P], AX.X, ALU.max, negate=True)
                        dve.tensor_reduce(nmax[:, s % 4, 1:2], sc[:, P:3 * P], AX.X, ALU.max,
                                          negate=True).then_inc(nmax_ready, 1)
                    if s >= 3 and heads or s < 3 and later(b):
                        dve.wait_ge(pT_ready, H - 2)
                        hb = (s - 3) % NPT
                        if later(b) or s - 3 >= NPT:
                            dve.wait_ge(out_ready, b * G0 + (s - 3) // G0 - 1)
                        dve.tensor_copy(pT[:, hb, :], T_BANK[:, 0:384]).then_inc(pT_taken, 1)
                    if s == 1 and later(b):
                        dve.wait_ge(probs_ready, b * NH)
                        invert(1)
                    if s == 9 and heads:
                        dve.wait_ge(probs_ready, b * NH + 8)
                        invert(0)
                    if s == DVE_A["stats"] and front:
                        dve.wait_ge(root_ready, b + 1)
                        step.hold()
                        stats(tile_of(b + 1), st, mv).then_inc(stats_ready, 1)
                    if s == DVE_A["normalise"] and front:
                        normalise(b + 1)
                    if s == DVE_A["expert_rows"] and post:
                        expert_rows(b - 1)
                    for f, job, bt in due(SCHED_A, s, b, post, heads, front):
                        (positions if job == "rank" else consume)(fam[f], job, bt)
                    if s == DVE_A["second_choice"] and post:
                        second_choice(b - 1)

            dve.wait_ge(x_loaded, 16)
            batch(0, False, True)
            with dve.Fori(1, B - 1) as b:
                step.loop(b - 1, 22)
                batch(b, True, True)
            step.end(B - 2)
            batch(B - 1, True, False)
            batch(B, True, False, heads=False)

            dve.tensor_copy(padi[:], base[0:1, :]).then_inc(tables_done, 1)
            dve.wait_ge(tables_done, 1)
            cnt, tiles, ends = small[:, 40:48], small[:, 48:56], small[:, 56:64]
            ends2 = small[:, 64:72]
            nxt, rof = small[:, 72:112], small[:, 112:152]
            for e in range(E):
                ins = dve.tensor_scalar(cnt[:, e:e + 1], base[:, e:e + 1], float(CAP * e), None, ALU.subtract)
            step.done(ins)
            t16 = tab[:, 0:E * 16].rearrange("p (e j) -> p e j", j=16)
            step.done(dve.tensor_tensor(t16, cnt.unsqueeze(2).broadcast_to([P, E, 16]), t16, ALU.is_gt))
            step.done(dve.tensor_reduce(tiles, t16, AX.X, ALU.add))
            src, dst = tiles, ends
            for sh in (1, 2, 4):
                step.done(dve.tensor_copy(dst[:, 0:sh], src[:, 0:sh]))
                step.done(dve.tensor_tensor(dst[:, sh:E], src[:, sh:E], src[:, 0:E - sh], ALU.add))
                src, dst = dst, (ends2 if dst is ends else ends)
            past = tab2[:].rearrange("p (i e) -> p i e", e=E)
            step.done(dve.tensor_tensor(past, past, src.unsqueeze(1).broadcast_to([P, 40, E]), ALU.is_ge))
            step.done(dve.tensor_reduce(nxt, past, AX.X, ALU.add))
            pt = tab[:].rearrange("p (i e) -> p i e", e=E)
            step.done(dve.tensor_tensor(pt, past, tiles.unsqueeze(1).broadcast_to([P, 40, E]), ALU.mult))
            step.done(dve.tensor_reduce(rof, pt, AX.X, ALU.add))
            step.done(dve.scalar_tensor_tensor(out=rof, in0=rof, scalar=-float(P), in1=small[:, 0:40],
                                               op0=ALU.mult, op1=ALU.add))
            step.done(dve.scalar_tensor_tensor(out=rof, in0=nxt, scalar=float(CAP), in1=rof,
                                               op0=ALU.mult, op1=ALU.add))
            step.done(dve.tensor_scalar(rof, rof, float(PAD_ROW), None, ALU.min))
            step.done(dve.tensor_scalar(nxt, nxt, float(E - 1), None, ALU.min))
            dve.tensor_copy(row_tab[:], rof[0:1, :])
            dve.tensor_copy(exp_tab[:], nxt[0:1, :]).then_inc(mixes_done, 1)
            move = small[:, 40:48]
            moved = tab2[:, 0:2 * NT * E].rearrange("p (i e) -> p i e", e=E)
            all_rows = pos_all[:].rearrange("p c t -> p (c t)")
            dve.tensor_copy(moved[:, :, E - 1], all_rows)
            step.done(dve.tensor_scalar(move, tiles, float(P), float(CAP), ALU.mult, ALU.subtract))
            for e in range(1, E):
                ins = dve.tensor_scalar(moved[:, :, e - 1], moved[:, :, E - 1], float(CAP * e), move[:, e - 1:e],
                                        ALU.is_ge, ALU.mult)
            step.done(ins)
            step.done(dve.tensor_reduce(small[:, 112:144], moved, AX.X, ALU.add))
            step.done(dve.tensor_copy(all_rows, small[:, 112:144]))
            dve.wait_ge(mixes_done, 2)
            step.done(dve.tensor_scalar(mix[:, 0, :], gap[:], 1.0, None, ALU.add))
            step.done(dve.reciprocal(mix[:, 0, :], mix[:, 0, :]))
            step.done(dve.tensor_scalar(mix[:, 0, :], mix[:, 0, :], gates[:, 2:3], None, ALU.mult))
            step.done(dve.tensor_tensor(mix[:, 1, :], mix[:, 0, :], gap[:], ALU.mult))

        @block.tensor
        def _(pe):
            mm = pe.matmul

            def fill(f, job, bt):
                r = f.bank(job)
                f.wait_free(pe, job, bt)
                if job == "xT":
                    pe.wait_ge(xn_ready, bt + 1)
                    for c in range(DC):
                        for t in range(TT):
                            o = c * S + t * P
                            ins = pe.transpose(r[:, o:o + P], xn[:, t, c * P:c * P + P], ident[:])
                if job in ("qk0", "qk1"):
                    c = int(job[2])
                    f.wait_other(pe, job, "xT", bt)
                    pe.wait_ge(ctx_loaded, bt * 16 + 16)
                    for j, (w, a) in enumerate(((wq, xnT), (wk, cT))):
                        for d in range(DC):
                            ins = mm(r[:, j * S:j * S + S], w[:, d, c * P:c * P + P], a[:, d, :],
                                     start=d == 0, stop=d == DC - 1)
                if job in ("v0", "v1"):
                    c = int(job[1])
                    pe.wait_ge(ctx_loaded, bt * 16 + 16)
                    for t in range(TT):
                        for d in range(DC):
                            ins = mm(r[:, t * P:t * P + P], cT[:, d, t * P:t * P + P], wv[:, d, c * P:c * P + P],
                                     start=d == 0, stop=d == DC - 1)
                if job == "rT":
                    pe.wait_ge(rinv_ready, bt * 2 + 2)
                    for t in range(TT):
                        ins = mm(r[0:NH, t * P:t * P + P], rinv[:, t, :], ident[:], start=True, stop=True)
                if job in ("bc0", "bc1"):
                    j = int(job[2])
                    f.wait_other(pe, job, "rT", bt)
                    for i in range(2):
                        ins = mm(r[:, i * S:i * S + S], sel[:, 2 * j + i, :], rT[:], start=True, stop=True)
                if job in ("wo0", "wo1"):
                    t = int(job[2])
                    for g in range(G0):
                        ins = mm(r[:, 0:D], oTn[:, g, t * P:t * P + P], wo[:, g, :], start=g == 0, stop=g == G0 - 1)
                if job == "x2T":
                    pe.wait_ge(xs_ready, bt + 1)
                    for c in range(DC):
                        for t in range(TT):
                            o = c * S + t * P
                            ins = pe.transpose(r[:, o:o + P], xs[:, t, c * P:c * P + P], ident[:])
                if job == "rt":
                    f.wait_other(pe, job, "x2T", bt)
                    for t in range(TT):
                        for c in range(DC):
                            ins = mm(r[:, t * E:t * E + E], x2T[:, c, t * P:t * P + P], wr[:, c, :],
                                     start=c == 0, stop=c == DC - 1)
                if job == "rank":
                    pe.wait_ge(hot_ready, bt + 1)
                    mm(r[:, 0:E], tri[:], hot[:, 0:E], start=True, stop=True)
                    mm(r[:, E:2 * E], tri[:], hot[:, E:2 * E], start=True, stop=False)
                    mm(r[:, E:2 * E], ones[:], hot[:, 0:E], start=False, stop=True)
                    mm(r[:, 2 * E:3 * E], ones[:], hot[:, 0:E], start=True, stop=False)
                    ins = mm(r[:, 2 * E:3 * E], ones[:], hot[:, E:2 * E], start=False, stop=True)
                ins.then_inc(f.ready_of(job), 1)

            pe.wait_ge(consts_done, CONSTS)
            pe.wait_ge(w_loaded, 96)
            pe.wait_ge(bvb_done, 1)
            for g in range(G0):
                ins = mm(fam["post"].bank("rT")[:, 0:D], bvb[:, g, :], wo[:, g, :], start=g == 0, stop=g == G0 - 1)
            ins.then_inc(crow_ready, 1)
            for job in ("xT", "qk0", "v0"):
                fill(fam["proj"], job, 0)

            def turn(b, s):
                pe.wait_ge(probs_ready, b * NH + s - 2)
                if later(b) or s >= 4:
                    pe.wait_ge(pT_taken, b * NH + s - 3)
                o, p = T_BANK, prob[:, (s - 3) % 4, :]
                pe.transpose(o[:, 0:P], p[:, 0:P], ident[:])
                pe.transpose(o[:, P:2 * P], p[:, P:2 * P], ident[:])
                pe.transpose(o[:, 2 * P:3 * P], p[:, 2 * P:3 * P], ident[:]).then_inc(pT_ready, 1)

            def scores(b, s):
                H = b * NH + s
                c = s // 8
                if s % 8 == 0:
                    fam["proj"].wait_taken(pe, f"qk{c}", b)
                pe.wait_ge(qz_ready, H + 1)
                if later(b) or s >= 4:
                    pe.wait_ge(probs_ready, H - 3)
                q, k, o = qz[:, s % 8, :], kT[:, c, :], S_BANK[s % 4]
                for t, (o0, o1) in enumerate(((0, P), (P, 3 * P))):
                    keys, q0 = o1 - o0, t * P
                    mm(o[:, o0:o1 - CHUNK], q[:, q0:q0 + P], k[:, 0:keys - CHUNK], start=True, stop=True)
                    ins = mm(o[CHUNK:P, o1 - CHUNK:o1], q[:, q0 + CHUNK:q0 + P], k[:, keys - CHUNK:keys], start=True, stop=True)
                ins.then_inc(scores_ready, 1)

            def values(b, s):
                g = (s - 4) % NH // G0
                G = b * G0 + (s - 4) // G0
                pe.wait_ge(pT_taken, b * NH + s - 3)
                if later(b) or g >= 1:
                    pe.wait_ge(out_taken, G)
                if g % 2 == 0:
                    fam["proj"].wait_taken(pe, f"v{g // 2}", b)
                o = O_BANK
                for kt in range(TT):
                    for j in range(G0):
                        h = g * G0 + j
                        pj = pT[:, h % NPT, :]
                        ins = mm(o[SLOT0 * j:SLOT0 * (j + 1), kt * P:S], V[:, kt, h, :],
                                 pj[:, 0:S] if kt == 0 else pj[:, S:S + P], start=kt == 0, stop=kt == 1)
                ins.then_inc(out_ready, 1)

            def batch(b, post, front, heads=True):
                for s in range(NH):
                    if heads:
                        scores(b, s)
                    if s >= 3 and heads or s < 3 and later(b):
                        turn(b, s)
                    for f, job, bt in due(SCHED_A, s, b, post, heads, front):
                        fill(fam[f], job, bt)
                    if s % G0 == G0 - 1 and (s >= 4 and heads or s < 4 and later(b)):
                        values(b, s)

            batch(0, False, True)
            pe.wait_ge(sel_done, 1)
            with pe.Fori(1, B - 1) as b:
                batch(b, True, True)
            batch(B - 1, True, False)
            batch(B, True, False, heads=False)


def later(b):
    return not isinstance(b, int) or b > 0


def phase_b(nc, v):
    with ExitStack() as ctx:
        experts_program(nc, v, ctx)


def experts_program(nc, v, ctx):
    bank, ident, ns, row_tab, exp_tab = (v[k] for k in ("bank", "ident", "ns", "row_tab", "exp_tab"))
    w_up, w_dn, rows_in, rows_out = (v[k] for k in ("w_up", "w_dn", "rows_in", "rows_out"))
    sb = lambda name, shape, dt=F32: ctx.enter_context(nc.sbuf_tensor(name, shape, dt))
    sem = lambda name: ctx.enter_context(nc.semaphore(name))
    xg = sb("xg", [P, 2, D])
    xgT = sb("xgT", [P, 2, DC * P])
    sg = sb("sg", [P, 2, HID])
    hh = sb("hh", [P, 2, HID])
    hT = sb("hT", [P, 2, HID])
    yy = sb("yy", [P, 2, D])
    loaded = [sem("rows0_loaded"), sem("rows1_loaded")]
    stored = [sem("rows0_stored"), sem("rows1_stored")]
    xT_ready, xT_taken, up_ready, silu_ready, h_ready = (sem(n) for n in (
        "moe_xT_ready", "moe_xT_taken", "moe_up_ready", "moe_silu_ready", "moe_h_ready"))
    hT_ready, hT_taken, y_ready, y_taken = (sem(n) for n in ("moe_hT_ready", "moe_hT_taken", "moe_y_ready", "moe_y_taken"))
    X_BANK, U_BANK, GATE_BANK, HT_BANK, Y_BANK = bank[0], bank[1:3], bank[3:5], bank[5:7], bank[7]
    LOOPED = TILES - 3
    assert LOOPED % 2 == 0

    def tiles(eng, slot):
        slot(0, 0, 0)
        with eng.Fori(0, LOOPED // 2) as t:
            slot(t * 2 + 1, 1, t)
            slot(t * 2 + 2, 0, t + 1)
        for i in range(LOOPED + 1, TILES):
            slot(i, i % 2, i // 2)

    def exists(i):
        return not isinstance(i, int) or i < TILES

    block = ctx.enter_context(nc.Block())

    @block.sync
    def _(sp):
        def load(i, u, t):
            row = sp.value_load(row_tab[0:1, bass.ds(i, 1)], min_val=0, max_val=PAD_ROW)
            sp.dma_start(xg[:, u, :], rows_in[bass.ds(row, P), :]).then_inc(loaded[u], 16)

        load(0, 0, 0)
        load(1, 1, 0)
        w = v["w"]
        for dst, src in ((w["wq"][:], v["Wq1"].rearrange("(c p) n -> p c n", p=P)),
                         (w["wk"][:], v["Wkv1"].rearrange("(c p) n -> p c n", p=P)[:, :, 0:NH * HD1]),
                         (w["gb"][:], v["gate_b"].partition_broadcast(P)),
                         (w["crow1"][:], v["bo1"].partition_broadcast(P)),
                         (w["crow3"][:], v["bo3"].partition_broadcast(P)),
                         (w["bi"][:], v["bi"].rearrange("(c p) -> p c", p=P))):
            sp.dma_start(dst, src).then_inc(v["w1_loaded"], 16)

        def slot(i, u, t):
            if exists(i + 2):
                sp.wait_ge(xT_ready, i + 1 + 2)
                load(i + 2, u, t + 1)
            if later(i):
                store(i - 1, 1 - u)

        def store(i, u):
            sp.wait_ge(y_taken, i + 1 + 2)
            sp.dma_start(rows_out[bass.ds(i * P, P), :], yy[:, u, :]).then_inc(stored[u], 16)

        tiles(sp, slot)
        store(TILES - 1, (TILES - 1) % 2)
        for u in range(2):
            sp.wait_ge(stored[u], 16 * (1 + (TILES + 1 - u) // 2))

    @block.scalar
    def _(act):
        for k in (xT_ready, xT_taken, up_ready, silu_ready, h_ready, hT_ready, hT_taken, y_ready, y_taken):
            act.sem_inc(k, 2)
        for k in stored:
            act.sem_inc(k, 16)

        def take_x(i, u):
            act.wait_ge(xT_ready, i + 1 + 2)
            for c in range(DC):
                ins = act.mul(xgT[:, u, c * P:c * P + P], X_BANK[:, c * P:c * P + P], ns[:, c:c + 1])
            ins.then_inc(xT_taken, 1)

        def silu(i, u):
            act.wait_ge(up_ready, i + 1 + 2)
            act.wait_ge(h_ready, i - 1 + 2)
            act.activation(sg[:, u, :], GATE_BANK[u][:], ACT.Silu).then_inc(silu_ready, 1)

        take_x(0, 0)
        silu(0, 0)
        take_x(1, 1)

        def slot(i, u, t):
            if exists(i + 1):
                silu(i + 1, 1 - u)
            if exists(i + 2):
                take_x(i + 2, u)
            act.wait_ge(y_ready, i + 1 + 2)
            act.wait_ge(stored[u], t * 16 + 16)
            act.copy(yy[:, u, :], Y_BANK[:, 0:D]).then_inc(y_taken, 1)

        tiles(act, slot)

    @block.vector
    def _(dve):
        def gated(i, u):
            dve.wait_ge(silu_ready, i + 1 + 2)
            dve.tensor_tensor(hh[:, u, :], U_BANK[u][:], sg[:, u, :], ALU.mult).then_inc(h_ready, 1)

        gated(0, 0)

        def slot(i, u, t):
            dve.wait_ge(hT_ready, i + 1 + 2)
            dve.wait_ge(y_ready, i - 1 + 2)
            dve.tensor_copy(hT[:, u, :], HT_BANK[u][:]).then_inc(hT_taken, 1)
            if exists(i + 1):
                gated(i + 1, 1 - u)

        tiles(dve, slot)

    @block.tensor
    def _(pe):
        def turn_x(i, u, t):
            pe.wait_ge(loaded[u], t * 16 + 16)
            pe.wait_ge(xT_taken, i + 2)
            for c in range(DC):
                ins = pe.transpose(X_BANK[:, c * P:c * P + P], xg[:, u, c * P:c * P + P], ident[:])
            ins.then_inc(xT_ready, 1)

        def up(i, u, e):
            pe.wait_ge(xT_taken, i + 1 + 2)
            pe.wait_ge(h_ready, i - 1 + 2)
            for half, o in ((1, GATE_BANK[u]), (0, U_BANK[u])):
                for c in range(DC):
                    ins = pe.matmul(o[:], xgT[:, u, c * P:c * P + P],
                                    w_up[:, bass.ds(e * (DC * 2 * HID) + (c * 2 * HID + half * HID), HID)],
                                    start=c == 0, stop=c == DC - 1)
            ins.then_inc(up_ready, 1)

        def expert(i):
            return pe.value_load(exp_tab[0:1, bass.ds(i, 1)], min_val=0, max_val=E - 1)

        def down(i, u, e):
            pe.wait_ge(hT_taken, i + 1 + 2)
            pe.wait_ge(y_taken, i + 2)
            for c in range(HC):
                ins = pe.matmul(Y_BANK[:, 0:D], hT[:, u, c * P:c * P + P],
                                w_dn[:, bass.ds(e * (HC * D) + c * D, D)], start=c == 0, stop=c == HC - 1)
            ins.then_inc(y_ready, 1)

        pe.wait_ge(v["moe_loaded"], 16 * 2 * E)
        pe.wait_ge(y_taken, 2)
        turn_x(0, 0, 0)
        up(0, 0, expert(0))
        turn_x(1, 1, 0)

        def slot(i, u, t):
            e, e1 = expert(i), expert(i + 1) if exists(i + 1) else None
            pe.wait_ge(h_ready, i + 1 + 2)
            pe.wait_ge(hT_taken, i - 1 + 2)
            for c in range(HC):
                ins = pe.transpose(HT_BANK[u][:, c * P:c * P + P], hh[:, u, c * P:c * P + P], ident[:])
            ins.then_inc(hT_ready, 1)
            if exists(i + 1):
                up(i + 1, 1 - u, e1)
            if exists(i + 2):
                turn_x(i + 2, u, t + 1)
            down(i, u, e)

        tiles(pe, slot)


def phase_c(nc, v):
    with ExitStack() as ctx:
        layer1_program(nc, v, ctx)


def layer1_program(nc, v, ctx):
    w, w1_loaded = v["w"], v["w1_loaded"]
    x_all, bank, ident, gates, nhalf = (v[k] for k in ("x_all", "bank", "ident", "gates", "nhalf"))
    mix, pos_all, rows_out, ctxT, out = (v[k] for k in ("mix", "pos_all", "rows_out", "ctxT", "out"))
    wq, wk, gb, crow, crow3, bi = (w[k] for k in ("wq", "wk", "gb", "crow1", "crow3", "bi"))
    sb = lambda name, shape, dt=F32: ctx.enter_context(nc.sbuf_tensor(name, shape, dt))
    sem = lambda name: ctx.enter_context(nc.semaphore(name))
    NP1 = NH // G1
    NPT1 = 4

    def split(name, *dims):
        return tuple(sb(name + part, [P] + list(dims), F32R)[:] for part in ("_hi", "_lo"))

    oT = wq[:].rearrange("p c n -> p (c n)").rearrange("p (g s) -> p g s", g=NP1)
    wv = sb("wv1", [P, DC, NH * HD1])
    oTn, pT = (a[:].rearrange("p c n -> p (c n)").rearrange("p (g s) -> p g s", g=g) for a, g in ((wk, NP1), (wv, NPT1)))
    wo, wd = sb("wo1", [P, NP1, D]), sb("wd1", [P, FC, D])
    wqs, wks, wvs = (split(n, DC, NH * HD1) for n in ("wq", "wk", "wv"))
    wis, lBs, lgs = split("wi", DC, FF), split("lB", FF), split("lg", DC, LG)
    xnT, cTs, x3T, amT = (split(n, DC, S) for n in ("xnT1", "cT1", "x3T", "amT"))
    qk = split("qk1", 2, 2 * S)
    hT = sb("hT1", [P, FC, S])[:]
    prob = sb("prob1", [P, 4, 2 * S])[:]
    V = sb("V1", [P, 2, TT, 2 * P])[:]
    yg = sb("yg", [P, 2, TT, D])[:]
    xn, cT, x3n = sb("xn1", [P, TT, D])[:], sb("cT_raw", [P, DC, S])[:], sb("x3n", [P, TT, D])[:]
    am = sb("am", [P, TT, 2, P])[:]
    base = sb("base1", [P, 2, S])[:]
    pre = sb("pre", [P, 2, 2, S])[:]
    xq, xp, ob = sb("xq", [P, TT, D])[:], sb("xp1", [P, TT, D])[:], sb("ob", [P, TT, D])[:]
    wi = hT.rearrange("p c s -> p (c s)").rearrange("p (c n) -> p c n", c=DC)
    lB = pre.rearrange("p a c n -> p (a c n)")
    lg_w = am.rearrange("p t c n -> p (t c n)")[:, 0:DC * LG].rearrange("p (c n) -> p c n", c=DC)
    zeros = prob[0:3 * NH, 0:2].rearrange("p b s -> p (b s)")
    one_sel = V[0:NH].rearrange("p a t d -> p (a t d)").rearrange("p (g s) -> p g s", g=NP1)
    sel = sb("sel1", [3 * NH, NP1, P], F32R)
    nmax = sb("nmax1", [P, 4, TT])
    den = sb("den1", [P, TT, NH])
    rinv = sb("rinv1", [P, TT, NH])
    rT = sb("rT1", [3 * NH, S], F32R)
    st = sb("st1", [P, TT, 6])
    mv = sb("mv1", [P, TT, 2])
    st2 = sb("st12", [P, TT, 6])
    mv2 = sb("mv12", [P, TT, 2])
    lnw = sb("lnw1", [P, 2, TT])
    lnw2 = sb("lnw12", [P, 2, TT])
    rev = sb("rev1", [P, TT, E])
    lg = sb("lg1", [P, TT, E])
    pr = sb("pr1", [P, TT, E])
    rw = sb("rw1", [P, 2, TT * E])
    r1 = sb("r11", [P, 6, TT])
    oh = sb("oh1", [P, 2, TT * E])
    gate = sb("gate", [P, TT])
    idx4 = sb("idx4", [P, 2, TT], U32)

    wv_loaded, ffn_loaded, out_loaded = sem("wv_loaded"), sem("ffn_loaded"), sem("out_loaded")
    ctx_loaded, gathered = sem("ctx_loaded1"), sem("gathered")
    weights_hi, weights_split, weights_late = sem("weights_hi"), sem("weights_split"), sem("weights_late")
    xT_hi, qk_hi, cT_hi, x3T_hi, amT_hi = (sem(n) for n in ("xT_hi", "qk_hi", "cT_hi", "x3T_hi", "amT_hi"))
    cT_split, sel_done, skip_ready = sem("cT_split"), sem("sel_done"), sem("skip_ready")
    consts_done, weights_done = sem("consts_done1"), sem("weights_done")
    scores_ready, nmax_ready, probs_ready = sem("scores_ready1"), sem("nmax_ready1"), sem("probs_ready1")
    pT_ready, pT_taken = sem("pT_ready1"), sem("pT_taken1")
    out_ready, out_taken, rinv_ready = sem("out_ready1"), sem("out_taken1"), sem("rinv_ready1")
    xq_ready, stats_ready, root_ready, xn_ready, x_shifted = (sem(n) for n in (
        "xq_ready", "stats_ready1", "root_ready1", "xn_ready1", "x_shifted1"))
    stats2_ready, root2_ready, x3_ready = sem("stats2_ready1"), sem("root2_ready1"), sem("x3_ready")
    pre_ready, h_ready = sem("pre_ready"), sem("h_ready")
    shifted_ready, exp_ready, am_ready, relu_ready = (sem(n) for n in (
        "logits_shifted", "logits_exp", "am_ready", "relu_ready"))
    final_ready, final_stored = sem("final_ready"), sem("final_stored")
    vec_step, pool_step = sem("vec_step_c"), sem("pool_step_c")
    S_BANK, T_BANK, O_BANK = bank[0:2], bank[2], bank[3]
    fam = {"proj": Family(PROJ_C, [bank[4]], [sem("proj_ready1")], [sem("proj_taken1")]),
           "post": Family(POST_C, [bank[5]], [sem("post_ready1")], [sem("post_taken1")]),
           "ffn": Family(FFN_C, bank[6:8], [sem("ffn0_ready"), sem("ffn1_ready")],
                         [sem("ffn0_taken"), sem("ffn1_taken")])}
    FFN_SPLIT = {4: (wis[0], wi), 6: (lBs[0], lB), 8: (lgs[0], lg_w)}
    W1_LOADS = 16 * 6
    block = ctx.enter_context(nc.Block())

    @block.sync
    def _(sp):
        cv = ctxT.rearrange("b (c p) s -> b p c s", p=P)
        ov = out.rearrange("b (t p) d -> b p t d", p=P)

        def context(b):
            sp.dma_start(cT, cv[bass.ds(b, 1)].rearrange("o p c s -> (o p) c s")).then_inc(ctx_loaded, 16)

        def next_context(b):
            sp.wait_ge(cT_split, b + 1)
            context(b + 1)

        def store(b):
            sp.wait_ge(final_ready, b + 1)
            sp.dma_start(ov[bass.ds(b, 1)].rearrange("o p t d -> (o p) t d"), ob).then_inc(final_stored, 16)

        context(0)
        sp.dma_start(wv[:], v["Wkv1"].rearrange("(c p) n -> p c n", p=P)[:, :, NH * HD1:2 * NH * HD1]).then_inc(wv_loaded, 16)
        sp.wait_ge(gathered, 32 * TT)
        sp.dma_start(wi, v["wiT"].rearrange("(c p) n -> p c n", p=P)).then_inc(ffn_loaded, 16)
        sp.dma_start(lB, v["loraB"]).then_inc(ffn_loaded, 16)
        sp.dma_start(lg_w[:, :, 0:E * R], v["loraAT"].rearrange("(c p) n -> p c n", p=P)).then_inc(ffn_loaded, 16)
        sp.dma_start(lg_w[:, :, E * R:LG], v["gate_wT"].rearrange("(c p) n -> p c n", p=P)).then_inc(ffn_loaded, 16)
        sp.dma_start(wo[:], v["Wo1"].rearrange("(c p) n -> p c n", p=P)).then_inc(out_loaded, 16)
        sp.dma_start(wd[:], v["woT"].rearrange("(c p) n -> p c n", p=P)).then_inc(out_loaded, 16)
        next_context(0)
        next_context(1)
        with sp.Fori(2, B - 1) as b:
            next_context(b)
            store(b - 2)
        for b in range(B - 3, B):
            store(b)
        sp.wait_ge(final_stored, 16 * (B + 1))

    @block.gpsimd
    def _(pool):
        step = Steps(pool, pool_step)

        def gather(b1):
            if later(b1):
                pool.wait_ge(xq_ready, b1)
                step.hold()
            step.done(pool.tensor_copy(idx4[:], pos_all[:, :, bass.ds(b1 * TT, TT)]))
            step.hold()
            for c in range(2):
                for t in range(TT):
                    pool.indirect_dma_start(yg[:, c, t, :], None, rows_out,
                                            bass.IndirectOffsetOnAxis(ap=idx4[:, c, t:t + 1], axis=0)).then_inc(gathered, 16)

        def root(w, m, ready):
            step.hold()
            step.done(pool.tensor_scalar(w[:, 0, :], m[:, :, 1], LN_EPS, None, ALU.add))
            pool.tensor_tensor(w[:, 1, :], w[:, 0, :], nhalf[:], ALU.pow).then_inc(ready, 1)

        def front_root(b1):
            pool.wait_ge(stats_ready, b1 + 1)
            root(lnw, mv, root_ready)

        def front_shift(b1):
            pool.wait_ge(xn_ready, b1 + 1)
            step.hold()
            pool.tensor_tensor(x_all[:, bass.ds(b1 * TT, TT), :], xq,
                               crow[:].unsqueeze(1).broadcast_to([P, TT, D]), ALU.add).then_inc(x_shifted, 1)

        def post_root(b0):
            pool.wait_ge(stats2_ready, b0 + 1)
            root(lnw2, mv2, root2_ready)

        def post_skip(b0):
            pool.wait_ge(final_stored, b0 * 16 + 16)
            step.hold()
            pool.tensor_copy(ob, xp).then_inc(skip_ready, 1)

        def batch(b, tail, post, front):
            for s in range(NH):
                if s == 0 and front:
                    gather(b + 1)
                if s == 4 and front:
                    front_root(b + 1)
                if s == 7 and front:
                    front_shift(b + 1)
                if s == 8 and post:
                    post_root(b - 1)
                if s == 15 and post:
                    post_skip(b - 1)

        pool.wait_ge(w1_loaded, W1_LOADS)
        gather(0)
        step.done(pool.memset(one_sel, 1.0))
        sv = one_sel.rearrange("h g (j d) -> h g j d", j=G1)
        pool.affine_select(out=sv, in_=sv, compare_op=ALU.is_equal, fill=0.0, base=0,
                           pattern=[[-G1, NP1], [-1, G1], [0, HD1]], channel_multiplier=1).then_inc(sel_done, 1)
        pool.iota(rev[:], pattern=[[0, TT], [-1, E]], base=E, channel_multiplier=0,
                  allow_small_or_imprecise_dtypes=True).then_inc(consts_done, 1)
        front_root(0)
        pool.wait_ge(weights_done, 2)
        front_shift(0)
        batch(0, False, False, True)
        for i, ((hi, lo), raw) in enumerate(((wis, wi), (lBs, lB), (lgs, lg_w))):
            pool.wait_ge(weights_hi, 4 + i)
            pool.tensor_tensor(lo, raw, hi.bitcast(F32), ALU.subtract).then_inc(weights_late, 1)
        batch(1, False, True, True)
        with pool.Fori(2, B - 1) as b:
            step.loop(b - 2, 9)
            batch(b, True, True, True)
        step.end(B - 3)
        batch(B - 1, True, True, False)
        batch(B, True, True, False)
        batch(B + 1, True, False, False)

    @block.scalar
    def _(act):
        act.wait_ge(w1_loaded, W1_LOADS)
        act.mul(wqs[0], wq[:], HD1 ** -0.5).then_inc(weights_hi, 1)
        act.copy(wks[0], wk[:]).then_inc(weights_hi, 1)
        act.mul(crow3[:], crow3[:], 2.0).then_inc(weights_done, 1)
        act.mul(crow[:], crow[:], gates[:, 1:2]).then_inc(weights_done, 1)
        act.sem_inc(final_stored, 16)
        for f in fam.values():
            for k in f.taken:
                act.sem_inc(k, 1)

        def consume(f, job, bt):
            r = f.bank(job)
            if job[0:2] in ("xT", "x3", "qk", "la", "ba"):
                f.wait_ready(act, job, bt)
            if job == "x3T" and later(bt):
                fam["ffn"].wait_ready(act, f"base{FC // 2 - 1}", bt - 1)
            if job == "laT" and later(bt):
                fam["ffn"].wait_ready(act, f"lora{FC - 1}", bt - 1)
            if job == "xT":
                act.copy(xnT[0].rearrange("p c s -> p (c s)"), r[:]).then_inc(xT_hi, 1)
            if job == "x3T":
                act.copy(x3T[0].rearrange("p c s -> p (c s)"), r[:]).then_inc(x3T_hi, 1)
            if job == "laT":
                act.copy(amT[0].rearrange("p c s -> p (c s)"), r[:]).then_inc(amT_hi, 1)
            if job[0:2] == "qk":
                p = int(job[2])
                if p >= 2 or later(bt):
                    act.wait_ge(scores_ready, bt * NH + 2 * p - 2)
                act.copy(qk[0][:, p % 2, :], r[:]).then_inc(qk_hi, 1)
            if job == "rl":
                act.wait_ge(shifted_ready, bt + 1)
                act.activation(pr[:], lg[:], ACT.Exp).then_inc(exp_ready, 1)
            if job[0:4] == "base":
                g = int(job[4])
                if g >= 1 or later(bt):
                    act.wait_ge(pre_ready, bt * FC + 2 * g)
                for i in range(2):
                    c = 2 * g + i
                    ins = act.activation(base[:, i, :], r[:, i * S:i * S + S], ACT.Identity, bias=bi[:, c:c + 1])
                ins.then_inc(f.taken_of(job), 1)
            if job[0:4] == "lora":
                c = int(job[4])
                act.wait_ge(pre_ready, bt * FC + c + 1)
                act.activation(pre[:, c % 2, 1, :], pre[:, c % 2, 1, :], ACT.Relu).then_inc(relu_ready, 1)

        def context_hi(b):
            act.wait_ge(ctx_loaded, b * 16 + 16)
            if later(b):
                fam["proj"].wait_ready(act, "qk7", b - 1)
            act.copy(cTs[0], cT).then_inc(cT_hi, 1)

        context_hi(0)
        act.wait_ge(wv_loaded, 16)
        act.copy(wvs[0], wv[:]).then_inc(weights_hi, 1)
        consume(fam["proj"], "xT", 0)
        consume(fam["proj"], "qk0", 0)

        def batch(b, tail, post, front, heads=True):
            for s in range(NH):
                H = b * NH + s
                if heads:
                    if later(b) and s == 0:
                        act.wait_ge(rinv_ready, b * 2 - 1)
                    if later(b) and s == 8:
                        act.wait_ge(rinv_ready, b * 2)
                    act.wait_ge(nmax_ready, H + 1)
                    for t in range(TT):
                        ins = act.activation(prob[:, s % 4, t * S:t * S + S], S_BANK[s % 2][:, t * S:t * S + S], ACT.Exp,
                                             bias=nmax[:, s % 4, t:t + 1], accum_out=den[:, t, s:s + 1])
                    ins.then_inc(probs_ready, 1)
                if isinstance(b, int) and b == 0 and s in FFN_SPLIT:
                    hi, raw = FFN_SPLIT[s]
                    act.wait_ge(ffn_loaded, 64)
                    act.copy(hi, raw).then_inc(weights_hi, 1)
                if s == 13 and front:
                    context_hi(b + 1)
                for f, job, bt in due(SCHED_C, s, b, post, heads, front, tail):
                    consume(fam[f], job, bt)
                if s % G1 == 0 and (s >= 4 and heads or s < 4 and post):
                    g = (s - 4) % NH // G1
                    act.wait_ge(out_ready, b * NP1 + (s - 4) // G1 + 1)
                    if later(b) and s >= 4:
                        fam["post"].wait_taken(act, "bc0" if g < 2 else "bc1" if g < 4 else "bc3", b - 1)
                    act.copy(oT[:, g, :], O_BANK[:, 0:S]).then_inc(out_taken, 1)

        batch(0, False, False, True)
        batch(1, False, True, True)
        with act.Fori(2, B - 1) as b:
            batch(b, True, True, True)
        batch(B - 1, True, True, False)
        batch(B, True, True, False, heads=False)
        batch(B + 1, True, False, False, heads=False)

    @block.vector
    def _(dve):
        step = Steps(dve, vec_step)
        dve.wait_ge(w1_loaded, W1_LOADS)

        def te(a):
            return a.rearrange("p (t e) -> p t e", e=E)

        def stats(a, st_, mv_):
            for t in range(TT):
                ins = dve.bn_stats(st_[:, t, :], a[:, t, :])
            step.done(ins)
            step.hold()
            for t in range(TT):
                ins = dve.bn_aggr(mv_[:, t, :], st_[:, t, :])
            return ins

        def combine_first(b1):
            dve.wait_ge(gathered, b1 * (32 * TT) + 32 * TT)
            if later(b1):
                dve.wait_ge(x_shifted, b1)
            for t in range(TT):
                ins = dve.scalar_tensor_tensor(
                    out=xq[:, t, :], in0=yg[:, 0, t, :], scalar=mix[:, 0, bass.ds(b1 * TT + t, 1)],
                    in1=x_all[:, bass.ds(b1 * TT + t, 1), :].rearrange("p o d -> p (o d)"), op0=ALU.mult, op1=ALU.add)
            step.done(ins)

        def combine_second(b1):
            for t in range(TT):
                ins = dve.scalar_tensor_tensor(
                    out=xq[:, t, :], in0=yg[:, 1, t, :], scalar=mix[:, 1, bass.ds(b1 * TT + t, 1)],
                    in1=xq[:, t, :], op0=ALU.mult, op1=ALU.add)
            ins.then_inc(xq_ready, 1)

        def xq_stats(b1):
            dve.wait_ge(xq_ready, b1 + 1)
            step.hold()
            stats(xq, st, mv).then_inc(stats_ready, 1)

        def normalise(b1):
            dve.wait_ge(root_ready, b1 + 1)
            if later(b1):
                fam["proj"].wait_ready(dve, "xT", b1 - 1)
            for t in range(TT):
                ins = dve.tensor_scalar(xn[:, t, :], xq[:, t, :], mv[:, t, 0:1], lnw[:, 1, t:t + 1],
                                        ALU.subtract, ALU.mult)
            ins.then_inc(xn_ready, 1)

        def normalise3(b0):
            dve.wait_ge(root2_ready, b0 + 1)
            for t in range(TT):
                ins = dve.tensor_scalar(x3n[:, t, :], xp[:, t, :], mv2[:, t, 0:1], lnw2[:, 1, t:t + 1],
                                        ALU.subtract, ALU.mult)
            ins.then_inc(x3_ready, 1)

        def invert(half):
            h = slice(8 * half, 8 * half + 8)
            dve.reciprocal(rinv[:, :, h], den[:, :, h]).then_inc(rinv_ready, 1)

        def first_of(src, m, one):
            a = te(rw[:, 0, :])
            step.done(dve.tensor_reduce(m, src, AX.X, ALU.max))
            step.done(dve.tensor_tensor(a, src, m.unsqueeze(2).broadcast_to([P, TT, E]), ALU.is_equal))
            step.done(dve.tensor_tensor(a, a, rev[:], ALU.mult))
            step.done(dve.tensor_reduce(r1[:, 3, :], a, AX.X, ALU.max))
            step.done(dve.tensor_tensor(one, rev[:], r1[:, 3, :].unsqueeze(2).broadcast_to([P, TT, E]), ALU.is_equal))

        def choose_first(b0):
            dve.wait_ge(exp_ready, b0 + 1)
            step.done(dve.tensor_reduce(r1[:, 4, :], pr[:], AX.X, ALU.add))
            step.done(dve.reciprocal(r1[:, 4, :], r1[:, 4, :]))
            step.done(dve.tensor_tensor(pr[:], pr[:], r1[:, 4, :].unsqueeze(2).broadcast_to([P, TT, E]), ALU.mult))
            first_of(pr[:], r1[:, 0, :], te(oh[:, 0, :]))

        def choose_second():
            p2 = te(rw[:, 1, :])
            step.done(dve.scalar_tensor_tensor(out=p2, in0=te(oh[:, 0, :]), scalar=LOWER, in1=pr[:],
                                               op0=ALU.mult, op1=ALU.add))
            first_of(p2, r1[:, 1, :], te(oh[:, 1, :]))
            step.done(dve.tensor_tensor(r1[:, 2, :], r1[:, 0, :], r1[:, 1, :], ALU.add))
            step.done(dve.tensor_scalar(r1[:, 5, :], r1[:, 2, :], gates[:, 3:4], None, ALU.mult))

        def masked(bt):
            r = fam["post"].bank("rl")[:, 0:TT * LG].rearrange("p (t e) -> p t e", t=TT)
            for c in range(2):
                ins = dve.tensor_tensor(am[:, :, c, :].rearrange("p t (e r) -> p t e r", r=R),
                                        r[:, :, 0:E * R].rearrange("p t (e r) -> p t e r", r=R),
                                        te(oh[:, c, :]).unsqueeze(3).broadcast_to([P, TT, E, R]), ALU.mult)
            ins.then_inc(am_ready, 1)
            dve.wait_ge(am_ready, bt + 1)
            dve.sem_inc(fam["post"].taken_of("rl"), 1)

        def low(parts_, r, hi_ready, n, done):
            hi, lo = (a.rearrange("p c s -> p (c s)") for a in parts_)
            dve.wait_ge(hi_ready, n)
            dve.tensor_tensor(lo, r[:], hi.bitcast(F32), ALU.subtract).then_inc(done, 1)

        def add_relus(c, bt):
            dve.wait_ge(relu_ready, bt * FC + c + 1)
            dve.scalar_tensor_tensor(out=hT[:, c, :], in0=pre[:, c % 2, 0, :], scalar=0.0, in1=pre[:, c % 2, 1, :],
                                     op0=ALU.max, op1=ALU.add).then_inc(h_ready, 1)

        def context_low(b):
            low(cTs, cT.rearrange("p c s -> p (c s)"), cT_hi, b + 1, cT_split)

        def consume(f, job, bt):
            r = f.bank(job)
            taken = f.taken_of(job)
            if job[0] in "vbwr" or job[0:2] in ("lo", "do"):
                f.wait_ready(dve, job, bt)
            if job == "xT":
                low(xnT, r, xT_hi, bt + 1, taken)
            if job == "x3T":
                low(x3T, r, x3T_hi, bt + 1, taken)
            if job == "laT":
                low(amT, r, amT_hi, bt + 1, taken)
            if job[0:2] == "qk":
                p = int(job[2])
                dve.wait_ge(qk_hi, bt * NP1 + p + 1)
                dve.tensor_tensor(qk[1][:, p % 2, :], r[:], qk[0][:, p % 2, :].bitcast(F32), ALU.subtract).then_inc(taken, 1)
            if job[0] == "v":
                k = int(job[2])
                if k >= 2 or later(bt):
                    dve.wait_ge(out_ready, bt * NP1 + 2 * k - 2)
                dve.tensor_copy(V[:, k % 2, :, :], r[:].rearrange("p (t d) -> p t d", t=TT)).then_inc(taken, 1)
            if job == "rT":
                step.done(dve.tensor_copy(rT[0:NH], r[0:NH, 0:S]))
                dve.tensor_tensor(rT[2 * NH:3 * NH], r[0:NH, 0:S], rT[0:NH].bitcast(F32), ALU.subtract).then_inc(taken, 1)
            if job[0:2] == "bc":
                j = int(job[2])
                dve.wait_ge(out_taken, bt * NP1 + NP1)
                dve.tensor_tensor(oTn[:, 2 * j:2 * j + 2, :], oT[:, 2 * j:2 * j + 2, :],
                                  r[:].rearrange("p (g s) -> p g s", g=2), ALU.mult).then_inc(taken, 1)
            if job in ("wo0", "wo1"):
                t = int(job[2])
                dve.wait_ge(x_shifted, bt + 1)
                if t == 0 and later(bt):
                    dve.wait_ge(skip_ready, bt)
                dve.scalar_tensor_tensor(
                    out=xp[:, t, :], in0=r[:, 0:D], scalar=gates[:, 1:2],
                    in1=x_all[:, bass.ds(bt * TT + t, 1), :].rearrange("p o d -> p (o d)"), op0=ALU.mult,
                    op1=ALU.add).then_inc(taken, 1)
                f.wait_taken(dve, job, bt)
                step.done(dve.bn_stats(st2[:, t, :], xp[:, t, :]))
                step.hold()
                ins = dve.bn_aggr(mv2[:, t, :], st2[:, t, :])
                if t == TT - 1:
                    ins.then_inc(stats2_ready, 1)
            if job == "rl":
                step.done(dve.tensor_tensor(lg[:], r[:, 0:TT * LG].rearrange("p (t e) -> p t e", t=TT)[:, :, E * R:LG],
                                            gb[:].unsqueeze(1).broadcast_to([P, TT, E]), ALU.add))
                step.done(dve.tensor_reduce(r1[:, 4, :], lg[:], AX.X, ALU.max))
                dve.tensor_tensor(lg[:], lg[:], r1[:, 4, :].unsqueeze(2).broadcast_to([P, TT, E]),
                                  ALU.subtract).then_inc(shifted_ready, 1)
            if job[0:4] == "lora":
                c = int(job[4])
                f.wait_taken(dve, f"base{c // 2}", bt)
                if c >= 2:
                    dve.wait_ge(h_ready, bt * FC + c - 1)
                elif c == 0 and later(bt):
                    dve.wait_ge(final_ready, bt)
                dve.tensor_tensor(pre[:, c % 2], r[:].rearrange("p (e s) -> p e s", e=2),
                                  base[:, c % 2, :].unsqueeze(1).broadcast_to([P, 2, S]), ALU.add).then_inc(taken, 1)
                f.wait_taken(dve, job, bt)
                dve.sem_inc(pre_ready, 1)
                if c >= 1:
                    add_relus(c - 1, bt)
            if job in ("down0", "down1"):
                t = int(job[4])
                if t == 0:
                    dve.wait_ge(skip_ready, bt + 1)
                dve.tensor_tensor(pre[:, t, 0, :], r[:, 0:D], crow3[:], ALU.add).then_inc(taken, 1)
                f.wait_taken(dve, job, bt)
                ins = dve.scalar_tensor_tensor(out=ob[:, t, :], in0=pre[:, t, 0, :], scalar=gate[:, t:t + 1],
                                               in1=ob[:, t, :], op0=ALU.mult, op1=ALU.add)
                if t == TT - 1:
                    ins.then_inc(final_ready, 1)

        step.done(dve.memset(zeros, 0.0))
        dve.tensor_copy(rT[:], zeros[:, 0:S]).then_inc(consts_done, 1)
        step.done(dve.tensor_copy(sel[:], zeros.rearrange("p (g s) -> p g s", g=NP1)))
        dve.wait_ge(weights_hi, 1)
        dve.scalar_tensor_tensor(out=wqs[1], in0=wq[:], scalar=HD1 ** -0.5, in1=wqs[0].bitcast(F32), op0=ALU.mult,
                                 op1=ALU.subtract).then_inc(weights_split, 1)
        dve.wait_ge(weights_hi, 2)
        dve.tensor_tensor(wks[1], wk[:], wks[0].bitcast(F32), ALU.subtract).then_inc(weights_split, 1)
        combine_first(0)
        combine_second(0)
        xq_stats(0)
        normalise(0)
        context_low(0)
        consume(fam["proj"], "xT", 0)
        dve.wait_ge(weights_hi, 3)
        dve.tensor_tensor(wvs[1], wv[:], wvs[0].bitcast(F32), ALU.subtract).then_inc(weights_split, 1)
        consume(fam["proj"], "qk0", 0)
        dve.wait_ge(sel_done, 1)
        dve.tensor_copy(sel[0:NH], one_sel)
        dve.tensor_copy(sel[2 * NH:3 * NH], one_sel).then_inc(consts_done, 1)
        dve.wait_ge(weights_done, 2)
        dve.wait_ge(consts_done, 3)
        consume(fam["proj"], "vv0", 0)

        def batch(b, tail, post, front, heads=True):
            for s in range(NH):
                H = b * NH + s
                if heads:
                    dve.wait_ge(scores_ready, H + 1)
                    dve.tensor_reduce(nmax[:, s % 4, :], S_BANK[s % 2][:].rearrange("p (t k) -> p t k", t=TT), AX.X,
                                      ALU.max, negate=True).then_inc(nmax_ready, 1)
                if s >= 2 and heads or s < 2 and post:
                    dve.wait_ge(pT_ready, H - 1)
                    if later(b) or s - 2 >= NPT1:
                        dve.wait_ge(out_ready, b * NP1 + (s - 2) // G1 - 1)
                    dve.tensor_copy(pT[:, (s - 2) % NPT1, :], T_BANK[:]).then_inc(pT_taken, 1)
                if s == 1 and post:
                    dve.wait_ge(probs_ready, b * NH)
                    invert(1)
                if s == 9 and heads:
                    dve.wait_ge(probs_ready, b * NH + 8)
                    invert(0)
                if s == 8 and tail:
                    add_relus(FC - 1, b - 2)
                if s == DVE_C["normalise3"] and post:
                    normalise3(b - 1)
                if s == DVE_C["normalise"] and front:
                    normalise(b + 1)
                if s == DVE_C["choose_first"] and post:
                    choose_first(b - 1)
                if s == 14 and post:
                    if tail:
                        dve.wait_ge(final_ready, b - 1)
                    step.done(dve.tensor_copy(gate[:], r1[:, 5, :]))
                for f, job, bt in due(SCHED_C, s, b, post, heads, front, tail):
                    consume(fam[f], job, bt)
                if s == DVE_C["combine_first"] and front:
                    combine_first(b + 1)
                if s == DVE_C["combine_second"] and front:
                    combine_second(b + 1)
                if s == DVE_C["stats"] and front:
                    xq_stats(b + 1)
                if s == 13 and front:
                    context_low(b + 1)
                if s == 13 and post:
                    choose_second()
                    masked(b - 1)

        batch(0, False, False, True)
        batch(1, False, True, True)
        with dve.Fori(2, B - 1) as b:
            step.loop(b - 2, 28)
            batch(b, True, True, True)
        step.end(B - 3)
        batch(B - 1, True, True, False)
        batch(B, True, True, False, heads=False)
        batch(B + 1, True, False, False, heads=False)

    @block.tensor
    def _(pe):
        mm = pe.matmul
        pe.wait_ge(w1_loaded, W1_LOADS)

        def product(o, terms):
            passes = [(st_[i][(slice(None),) + si], mv_[j][(slice(None),) + mi])
                      for st_, si, mv_, mi in terms for i, j in ((0, 0), (1, 0), (0, 1))]
            for n, (lhs, rhs) in enumerate(passes):
                ins = mm(o, lhs, rhs, start=n == 0, stop=n == len(passes) - 1)
            return ins

        def fill(f, job, bt):
            r = f.bank(job)
            f.wait_free(pe, job, bt)
            if job == "xT":
                pe.wait_ge(xn_ready, bt + 1)
            if job == "x3T":
                pe.wait_ge(x3_ready, bt + 1)
            if job in ("xT", "x3T"):
                a = xn if job == "xT" else x3n
                for c in range(DC):
                    for t in range(TT):
                        o = c * S + t * P
                        ins = pe.transpose(r[:, o:o + P], a[:, t, c * P:c * P + P], ident[:])
            if job[0:2] == "qk":
                p = int(job[2])
                pe.wait_ge(cT_split, bt + 1)
                for j, (wt, a) in enumerate(((wqs, xnT), (wks, cTs))):
                    ins = product(r[:, j * S:j * S + S], [(wt, (d, slice(p * P, p * P + P)), a, (d,)) for d in range(DC)])
            if job[0] == "v":
                k = int(job[2])
                pe.wait_ge(cT_split, bt + 1)
                o = k * 2 * P
                for t in range(TT):
                    ins = product(r[:, t * 2 * P:(t + 1) * 2 * P], [(cTs, (d, slice(t * P, t * P + P)), wvs,
                                                                     (d, slice(o, o + 2 * P))) for d in range(DC)])
            if job == "rT":
                pe.wait_ge(rinv_ready, bt * 2 + 2)
                for t in range(TT):
                    ins = mm(r[0:NH, t * P:t * P + P], rinv[:, t, :], ident[:], start=True, stop=True)
            if job[0:2] == "bc":
                j = int(job[2])
                f.wait_other(pe, job, "rT", bt)
                for i in range(2):
                    ins = mm(r[:, i * S:i * S + S], sel[:, 2 * j + i, :], rT[:], start=True, stop=True)
            if job in ("wo0", "wo1"):
                t = int(job[2])
                if t == 0:
                    f.wait_other(pe, job, "bc3", bt)
                for g in range(NP1):
                    ins = mm(r[:, 0:D], oTn[:, g, t * P:t * P + P], wo[:, g, :], start=g == 0, stop=g == NP1 - 1)
            if job == "rl":
                for t in range(TT):
                    ins = product(r[:, t * LG:t * LG + LG], [(x3T, (c, slice(t * P, t * P + P)), lgs, (c,))
                                                             for c in range(DC)])
            if job == "laT":
                pe.wait_ge(am_ready, bt + 1)
                for c in range(2):
                    for t in range(TT):
                        o = c * S + t * P
                        ins = pe.transpose(r[:, o:o + P], am[:, t, c, :], ident[:])
            if job[0:4] == "base":
                for i in range(2):
                    o = (2 * int(job[4]) + i) * P
                    ins = product(r[:, i * S:i * S + S], [(wis, (d, slice(o, o + P)), x3T, (d,)) for d in range(DC)])
            if job[0:4] == "lora":
                o = int(job[4]) * P
                if o == 0:
                    fam["post"].wait_taken(pe, "laT", bt)
                ins = product(r[:].rearrange("p (c s) -> p c s", c=2), [(lBs, (slice(o, o + P),), amT, ())])
            if job in ("down0", "down1"):
                t = int(job[4])
                if t == 0:
                    pe.wait_ge(h_ready, bt * FC + FC)
                for c in range(FC):
                    ins = mm(r[:, 0:D], hT[:, c, t * P:t * P + P], wd[:, c, :], start=c == 0, stop=c == FC - 1)
            ins.then_inc(f.ready_of(job), 1)

        pe.wait_ge(weights_done, 2)
        pe.wait_ge(weights_split, 2)
        for job in ("xT", "qk0", "vv0"):
            if job == "vv0":
                pe.wait_ge(weights_split, 3)
            fill(fam["proj"], job, 0)
        pe.wait_ge(consts_done, 3)

        def turn(b, s):
            if later(b) or s >= 3:
                pe.wait_ge(pT_taken, b * NH + s - 2)
            o, p = T_BANK, prob[:, (s - 2) % 4, :]
            for kt in range(TT):
                for t in range(TT):
                    ins = pe.transpose(o[:, kt * S + t * P:kt * S + t * P + P],
                                       p[:, t * S + kt * P:t * S + kt * P + P], ident[:])
            ins.then_inc(pT_ready, 1)

        def scores(b, s):
            p, j = s // 2, s % 2
            if j == 0:
                fam["proj"].wait_taken(pe, f"qk{p}", b)
            rows = slice(HD1 * j, HD1 * j + HD1)
            q, k = (tuple(a[rows, p % 2, o:o + S] for a in qk) for o in (0, S))
            for t in range(TT):
                ins = product(S_BANK[s % 2][:, t * S:t * S + S], [(q, (slice(t * P, t * P + P),), k, ())])
            ins.then_inc(scores_ready, 1)

        def values(b, s):
            g = (s - 4) % NH // G1
            G = b * NP1 + (s - 4) // G1
            pe.wait_ge(pT_taken, b * NH + s - 2)
            if later(b) or g >= 1:
                pe.wait_ge(out_taken, G)
            fam["proj"].wait_taken(pe, f"vv{g // 2}", b if s >= 4 else b - 1)
            for kt in range(TT):
                for j in range(G1):
                    ins = mm(O_BANK[HD1 * j:HD1 * j + HD1, 0:S], V[:, g // 2 % 2, kt, g % 2 * P + HD1 * j:g % 2 * P + HD1 * j + HD1],
                             pT[:, (2 * g + j) % NPT1, kt * S:kt * S + S], start=kt == 0, stop=kt == TT - 1)
            ins.then_inc(out_ready, 1)

        def batch(b, tail, post, front, heads=True):
            for s in range(NH):
                before = s >= 2 and heads or s < 2 and post
                if before:
                    pe.wait_ge(probs_ready, b * NH + s - 1)
                if heads:
                    scores(b, s)
                if before:
                    turn(b, s)
                for f, job, bt in due(SCHED_C, s, b, post, heads, front, tail):
                    fill(fam[f], job, bt)
                if s % G1 == 0 and (s >= 4 and heads or s < 4 and post):
                    values(b, s)

        batch(0, False, False, True)
        pe.wait_ge(weights_late, 3)
        pe.wait_ge(out_loaded, 32)
        batch(1, False, True, True)
        with pe.Fori(2, B - 1) as b:
            batch(b, True, True, True)
        batch(B - 1, True, True, False)
        batch(B, True, True, False, heads=False)
        batch(B + 1, True, False, False, heads=False)


_INS = ["x", "ctxT", "g_x", "g_f", "Wq0", "bq0", "Wk0", "bk0", "Wv0", "bv0", "Wo0", "bo0", "nscale", "w_routerT",
        "w_upT", "w_downT", "Wq1", "Wkv1", "Wo1", "bo1", "wiT", "bi", "woT", "bo3", "loraAT", "loraB", "gate_wT",
        "gate_b"]


def laid_out(i):
    t = lambda a, *axes: np.ascontiguousarray(np.transpose(np.asarray(a), axes or None))
    n = lambda a: np.ascontiguousarray(np.asarray(a))
    return dict(
        x=n(i["x"]), ctxT=t(i["ctx_1024"], 0, 2, 1), g_x=n(i["g_xattn"]), g_f=n(i["g_ffn"]),
        Wq0=n(i["L0_xattn_Wq"]), bq0=n(i["L0_xattn_bq"]), Wk0=n(i["L0_xattn_Wk"]), bk0=n(i["L0_xattn_bk"]),
        Wv0=n(i["L0_xattn_Wv"]), bv0=n(i["L0_xattn_bv"]), Wo0=n(i["L0_xattn_Wo"]), bo0=n(i["L0_xattn_bo"]),
        nscale=n(i["L0_ffn_norm_scale"]), w_routerT=t(i["L0_ffn_w_router"]),
        w_upT=t(i["L0_ffn_w_up"], 0, 2, 1), w_downT=t(i["L0_ffn_w_down"], 0, 2, 1),
        Wq1=n(i["L1_xattn_Wq"]), Wkv1=n(i["L1_xattn_Wkv"]), Wo1=n(i["L1_xattn_Wo"]), bo1=n(i["L1_xattn_bo"]),
        wiT=t(i["L1_ffn_wi"]), bi=n(i["L1_ffn_bi"]), woT=t(i["L1_ffn_wo"]), bo3=n(i["L1_ffn_bo"]),
        loraAT=t(np.reshape(np.asarray(i["L1_ffn_lora_A"]), (E * R, D))),
        loraB=np.reshape(t(i["L1_ffn_lora_B"], 0, 2, 1), (E * R, FF)),
        gate_wT=t(i["L1_ffn_gate_w"]), gate_b=n(i["L1_ffn_gate_b"]))


def kernel(**inputs):
    import concourse.bacc as bacc
    from concourse.bass_utils import run_bass_kernel_spmd

    nc = bacc.Bacc("TRN2", target_bir_lowering=False, num_devices=1)
    arrays = laid_out(inputs)
    args = [nc.dram_tensor(k, arrays[k].shape, mybir.dt.from_np(arrays[k].dtype), kind="ExternalInput").ap()
            for k in _INS]
    out = nc.dram_tensor("out", [B, S, D], F32, kind="ExternalOutput").ap()
    build(nc, *args, out)
    return run_bass_kernel_spmd(nc, [arrays], core_ids=[0]).results[0]["out"]
```
